# Optimizing a Trainium2 kernel written in Bass

```python
import numpy as np
import jax
import jax.numpy as jnp

def _softmax(x, axis=-1):
    return jax.nn.softmax(x, axis=axis)

def _gelu(x):
    return jax.nn.gelu(x, approximate=True)

def _silu(x):
    return jax.nn.silu(x)

def _sigmoid(x):
    return jax.nn.sigmoid(x)

def _layernorm(x, axis=-1, eps=1e-05):
    m = jnp.mean(x, axis=axis, keepdims=True)
    v = jnp.var(x, axis=axis, keepdims=True)
    return (x - m) / jnp.sqrt(v + eps)

def _scatter_add(tgt, idx, src, axis=0):
    return tgt.at[idx].add(src)

def _segment_sum(src, seg, n):
    return jax.ops.segment_sum(src, seg, n)
kernel_name = 'mk_adj_resnorm_d1_adj_r2_ecdd06'

def setup_inputs(seed: int=0):
    np.random.seed(seed)
    _w = jnp.asarray

    def _rec_inputs():
        import jax
        import jax.numpy as jnp
        _gk = jax.random.key(seed)
        x = 7.22e-05 + 1 * jax.random.normal(jax.random.fold_in(_gk, 1), (4096, 512), jnp.float32)
        _w = (1.0 + jnp.arange(4096, dtype=jnp.float32)) ** (-0.5)
        _w = _w / _w.mean()
        _pij = jnp.clip(0.000488281 * _w[:, None] * _w[None, :], 0.0, 1.0)
        _a = jax.random.uniform(jax.random.fold_in(_gk, 2), (4096, 4096)) < _pij
        _af = _a.astype(jnp.float32)
        adj = _af
        return (x, adj)
    x, adj = _rec_inputs()

    def _L0_gnn_setup():
        import jax, jax.numpy as jnp
        import numpy as np
        N = 4096
        D = 512
        key = jax.random.key(seed)
        ks = jax.random.split(key, 13)
        w_scale = 1.0 / np.sqrt(D)
        inp = {'query': jax.random.normal(ks[0], (N, D), dtype=jnp.float32), 'key': jax.random.normal(ks[1], (N, D), dtype=jnp.float32), 'value': jax.random.normal(ks[2], (N, D), dtype=jnp.float32), 'adj_matrix': jax.random.randint(ks[3], (N, N), 0, 2).astype(jnp.float32), 'Wq': jax.random.normal(ks[4], (D, D), dtype=jnp.float32) * w_scale, 'bq': jax.random.normal(ks[5], (D,), dtype=jnp.float32) * 0.01, 'Wk': jax.random.normal(ks[6], (D, D), dtype=jnp.float32) * w_scale, 'bk': jax.random.normal(ks[7], (D,), dtype=jnp.float32) * 0.01, 'Wv': jax.random.normal(ks[8], (D, D), dtype=jnp.float32) * w_scale, 'bv': jax.random.normal(ks[9], (D,), dtype=jnp.float32) * 0.01, 'Wm': jax.random.normal(ks[10], (D, D), dtype=jnp.float32) * w_scale, 'bm': jax.random.normal(ks[11], (D,), dtype=jnp.float32) * 0.01}
        return inp
    _L0_gnn_all = _L0_gnn_setup()
    _L0_gnn_in = {k: v for k, v in _L0_gnn_all.items() if k in ('key', 'value', 'Wq', 'bq', 'Wk', 'bk', 'Wv', 'bv', 'Wm', 'bm')}
    del _L0_gnn_all
    return {'x': x, 'adj': adj, 'L0_gnn_key': _L0_gnn_in['key'], 'L0_gnn_value': _L0_gnn_in['value'], 'L0_gnn_Wq': _L0_gnn_in['Wq'], 'L0_gnn_bq': _L0_gnn_in['bq'], 'L0_gnn_Wk': _L0_gnn_in['Wk'], 'L0_gnn_bk': _L0_gnn_in['bk'], 'L0_gnn_Wv': _L0_gnn_in['Wv'], 'L0_gnn_bv': _L0_gnn_in['bv'], 'L0_gnn_Wm': _L0_gnn_in['Wm'], 'L0_gnn_bm': _L0_gnn_in['bm']}

def reference(x, adj, L0_gnn_key, L0_gnn_value, L0_gnn_Wq, L0_gnn_bq, L0_gnn_Wk, L0_gnn_bk, L0_gnn_Wv, L0_gnn_bv, L0_gnn_Wm, L0_gnn_bm):
    import jax
    import jax.numpy as jnp

    def _L0_gnn_ref(query, key, value, adj_matrix, Wq, bq, Wk, bk, Wv, bv, Wm, bm):
        import jax, jax.numpy as jnp
        import numpy as np
        N = 4096
        D = 512
        q = query @ Wq.T + bq
        k = key @ Wk.T + bk
        v = value @ Wv.T + bv
        scale = q.shape[0] ** 0.5
        scores = jnp.einsum('nd,md->nm', q, k) / scale
        adj_scores = scores * adj_matrix
        adj_scores = jnp.where(jnp.abs(adj_scores) < 1e-05, -1000000000.0, adj_scores)
        prob = jax.nn.softmax(adj_scores, axis=-1)
        x = jnp.einsum('nm,md->nd', prob, v)
        return x @ Wm.T + bm
    x = _layernorm(x + _L0_gnn_ref(x, L0_gnn_key, L0_gnn_value, adj, L0_gnn_Wq, L0_gnn_bq, L0_gnn_Wk, L0_gnn_bk, L0_gnn_Wv, L0_gnn_bv, L0_gnn_Wm, L0_gnn_bm), axis=-1)
    return x

_drawn_inputs = setup_inputs


def setup_inputs(seed=0):
    import zlib

    import numpy as np

    out = dict(_drawn_inputs(seed))
    spreads = {}
    factors = {'L0_gnn_bq': 61.364, 'L0_gnn_bk': 64.0, 'L0_gnn_bv': 6.99, 'L0_gnn_bm': 6.509}
    for name, (base, spread) in spreads.items():
        noise = np.random.default_rng([zlib.crc32(name.encode()), seed]).standard_normal(out[name].shape)
        drawn = base * np.exp(spread * noise) if base else spread * noise
        out[name] = jnp.asarray(drawn.astype(out[name].dtype))
    for name, factor in factors.items():
        out[name] = (out[name] * factor).astype(out[name].dtype)
    return out
```

```python
from contextlib import ExitStack, contextmanager

import concourse.bass as bass
from concourse import mybir

F32 = mybir.dt.float32
BF16 = mybir.dt.bfloat16
I32 = mybir.dt.int32
ALU = mybir.AluOpType
ACT = mybir.ActivationFunctionType
AX_X = mybir.AxisListType.X

P = 128
N = 4096
D = 512
DC = D // P
T = N // P
HT = T // 2
G8 = P // HT
GK = N // G8
CH = 3
SLOTS = CH * P
GS = SLOTS // G8
SPC = P // G8
MAXR = -(-GK // GS)
NB = N // 512
HALVES = 2 * T
KV = 3
INV_SCALE = 1.0 / float(N) ** 0.5
MASKED = -1e9
TINY = 1e-5

C_ID = 0
C_DESC = C_ID + P
C_GRP = C_DESC + GK
C_SEL = C_GRP + P
C_BK = C_SEL + HT
C_BA = C_BK + 1
C_THR = C_BA + T
C_NEG = C_THR + MAXR
C_EPS = C_NEG + 1
C_B = C_EPS + 1
C_ALL = C_B + 3 * DC


@contextmanager
def strided(eng, start, stop, step):
    with eng.Fori(0, (stop - start) // step) as m:
        yield m * step + start


def build(nc, adj_tiles, adj_cols, kv_rows, value, x, xT, wq, wk, wv, wmT, bm, consts, out):
    with ExitStack() as ctx:
        def sb(name, shape, dt=F32):
            return ctx.enter_context(nc.sbuf_tensor(name, shape, dt))

        def sem(name):
            return ctx.enter_context(nc.semaphore(name))

        bank = [ctx.enter_context(nc.psum_tensor(f"bank{i}", [P, 512], F32)) for i in range(8)]

        cst = sb("cst", [P, C_ALL])
        ident = cst[:, C_ID:C_ID + P]
        descending = cst[:, C_DESC:C_DESC + GK]
        group_mask = cst[:, C_GRP:C_GRP + P].rearrange("p (g s) -> p g s", g=G8)
        tile_select = cst[:, C_SEL:C_SEL + HT]
        qT = sb("qT", [P, DC, N])
        G = sb("G", [P, DC, D])
        beta = sb("beta", [P, D])
        vsum = sb("vsum", [P, D])
        ones = sb("ones", [P, P])
        left = sb("left", [P, 2, GK])
        c_cols = sb("c_cols", [P, T])
        c_rows = sb("c_rows", [P, P])
        slots = sb("slots", [P, 2, GS])
        index = sb("index", [P, T, 2 * CH], I32)
        neg_max = sb("neg_max", [P, T])
        denom = sb("denom", [P, T])
        small = sb("small", [P, 64])
        rounds_i = sb("rounds_i", [1, 1], I32)

        O = sb("O", [P, T, D])
        o_flat = O[:, :, :].rearrange("p t d -> p (t d)")
        adj_buf = [o_flat[:, i * 2048:(i + 1) * 2048] for i in range(4)]
        joined = [o_flat[:, 8192 + i * 1024:8192 + (i + 1) * 1024].bitcast(BF16) for i in range(2)]
        xT_buf = [o_flat[:, 10240 + i * 2048:10240 + (i + 1) * 2048].rearrange("p (d n) -> p d n", d=DC)
                  for i in range(2)]
        v_buf = [o_flat[:, 14336 + i * 1024:14336 + (i + 1) * 1024] for i in range(2)]

        kv = sb("kv", [P, KV, CH, 2 * D])
        kv_flat = kv[:, :, :, :].rearrange("p b c d -> p (b c d)")
        w_left = kv_flat[:, 0:2048].rearrange("p (e d) -> p e d", e=DC)
        w_right = kv_flat[:, 2048:4096].rearrange("p (e d) -> p e d", e=DC)
        M = kv_flat[:, 4096:6144].rearrange("p (a d) -> p a d", a=DC)
        v_acc = kv_flat[:, 6144:7168]
        one_hot = kv_flat[:, 7168:7168 + 128].bitcast(BF16)
        u_col = kv_flat[:, 7296:7300]
        w_col = kv_flat[:, 7300:7304]
        kappa = kv_flat[:, 7304:7305]
        beta_row = kv_flat[0:1, 7344:7344 + D]
        bm_row = kv_flat[0:1, 7856:7856 + D]

        adj_g = sb("adj_g", [P, KV, CH, P])
        keyT = sb("keyT", [P, CH, D])
        zero_row = keyT[:, 2, :]
        prodT = sb("prodT", [P, 2, SLOTS])
        score = sb("score", [P, SLOTS])
        prob = sb("prob", [P, SLOTS])
        is_tiny = prob
        probT = sb("probT", [P, 2, SLOTS])
        c_diag = sb("c_diag", [P, 2, P])
        index_now = sb("index_now", [P, KV, 2 * CH], I32)
        chunk_max = sb("chunk_max", [P, 2])
        new_max = sb("new_max", [P, 2])
        alpha = sb("alpha", [P, 2])
        p_rest = sb("p_rest", [P, 2])
        p_sum = sb("p_sum", [P, 2])
        l_add = sb("l_add", [P, 2])
        spread = [prodT[:, i, 0:P].rearrange("p (g s) -> p g s", g=G8) for i in range(2)]

        x_buf = [kv_flat[:, i * 512:(i + 1) * 512] for i in range(4)]
        on_buf = [kv_flat[:, 3072 + i * 512:3072 + (i + 1) * 512] for i in range(2)]
        onT_buf = [kv_flat[:, 4096 + i * 512:4096 + (i + 1) * 512].rearrange("p (a r) -> p a r", a=DC)
                   for i in range(2)]
        y_buf = [kv_flat[:, 5120 + i * 512:5120 + (i + 1) * 512] for i in range(2)]
        fin_buf = [kv_flat[:, 6144 + i * 512:6144 + (i + 1) * 512] for i in range(2)]
        stats = kv_flat[:, 7168:7180].rearrange("p (b s) -> p b s", b=2)
        mean_var = kv_flat[:, 7184:7188].rearrange("p (b s) -> p b s", b=2)
        std = kv_flat[:, 7192:7194]
        rstd = kv_flat[:, 7200:7202]
        p_all = small[:, 0:T]
        r_denom = denom


        cst_in = sem("cst_in")
        passed = sem("passed")
        weights_in = sem("weights_in")
        weights2_in = sem("weights2_in")
        bm_in = sem("bm_in")
        filled = sem("filled")
        prep_ps = sem("prep_ps")
        prep_sb = sem("prep_sb")
        adj_in = [sem(f"adj_in{i}") for i in range(4)]
        xT_in = [sem(f"xT_in{i}") for i in range(2)]
        v_in = [sem(f"v_in{i}") for i in range(2)]
        v_added = sem("v_added")
        joined_sb = sem("joined_sb")
        joined_used = sem("joined_used")
        q_ps = sem("q_ps")
        q_sb = sem("q_sb")
        c_ps = sem("c_ps")
        c_sb = sem("c_sb")
        left_sb = sem("left_sb")
        lead_sb = sem("lead_sb")
        lead_ps = sem("lead_ps")
        kv_zeroed = sem("kv_zeroed")
        o_zeroed = sem("o_zeroed")
        rounds_ready = sem("rounds_ready")
        took = sem("took")
        spread_sb = sem("spread_sb")
        spread_ps = sem("spread_ps")
        index_ready = sem("index_ready")
        index_copied = sem("index_copied")
        gathered = [sem(f"gathered{i}") for i in range(KV)]
        keyT_ps = sem("keyT_ps")
        keyT_sb = sem("keyT_sb")
        c_ready = sem("c_ready")
        score_ps = sem("score_ps")
        prodT_sb = sem("prodT_sb")
        prod_ps = sem("prod_ps")
        abs_sb = sem("abs_sb")
        tiny_sb = sem("tiny_sb")
        masked = sem("masked")
        max_sb = sem("max_sb")
        new_max_sb = sem("new_max_sb")
        exp_sb = sem("exp_sb")
        weight_sb = sem("weight_sb")
        sum_sb = sem("sum_sb")
        state_sb = sem("state_sb")
        probT_ps = sem("probT_ps")
        probT_sb = sem("probT_sb")
        pv_ps = sem("pv_ps")
        o_sb = sem("o_sb")
        rest_sb = sem("rest_sb")
        end_sb = sem("end_sb")
        end_exp = sem("end_exp")
        end_l = sem("end_l")
        x_in = [sem(f"x_in{i}") for i in range(4)]
        xb_sb = sem("xb_sb")
        on_sb = sem("on_sb")
        onT_ps = sem("onT_ps")
        onT_sb = sem("onT_sb")
        y_ps = sem("y_ps")
        y_sb = sem("y_sb")
        stats_sb = sem("stats_sb")
        mean_sb = sem("mean_sb")
        std_sb = sem("std_sb")
        rstd_sb = sem("rstd_sb")
        fin_sb = sem("fin_sb")
        stored = [sem(f"stored{i}") for i in range(2)]

        FILLS = 9
        TAKES = 4 * GS // 8
        x_tiles = x.rearrange("(r t) d -> t r d", t=T)
        out_tiles = out.rearrange("(r t) d -> t r d", t=T)
        v_rows = value.rearrange("(b p k) d -> b p (k d)", p=P, k=2)

        def one(ap, i):
            return ap[bass.ds(i, 1)].rearrange("a p n -> p (a n)")

        def cols(ap, start, n):
            return ap[:, bass.ds(start, n)]

        def wait_apart(eng, s, value):
            eng.wait_ge(s, value)
            eng.sem_inc(passed, 1)

        def tile_steps(eng, step):
            step(0, 0, 0, True, False, False)
            step(1, 0, 1, True, True, False)
            with eng.Fori(0, (T - 2) // 6) as m:
                for j in range(6):
                    step(m * 6 + (2 + j), m * 2 + (2 + j) // KV, 2 + j, True, True, True)
            step(T, T // KV, T % 6, False, True, True)
            step(T + 1, (T + 1) // KV, (T + 1) % 6, False, False, True)

        def super_rounds(eng):
            eng.wait_ge(rounds_ready, 1)
            n = eng.value_load(rounds_i[0:1, 0:1], min_val=1, max_val=MAXR)
            return eng.Fori(0, n)

        IN_BUF = [len(range(b, T, KV)) for b in range(KV)]

        block = ctx.enter_context(nc.Block())

        @block.sync
        def _(sp):
            sp.dma_start(cst[:, :], consts).then_inc(cst_in, 16)
            sp.dma_start(w_left, wq.rearrange("(e p) d -> p e d", p=P)).then_inc(weights_in, 16)
            sp.dma_start(w_right, wk.rearrange("(e p) d -> p e d", p=P)).then_inc(weights_in, 16)
            sp.dma_start(bm_row, bm).then_inc(bm_in, 16)
            with strided(sp, 0, NB, 2) as nb:
                for j in range(2):
                    sp.wait_ge(c_ps, nb + (j + 1))
                    sp.dma_start(xT_buf[j], xT[bass.ds(nb + j, 1)].rearrange("a p d n -> p (a d) n")
                                 ).then_inc(xT_in[j], 16)
                    for i in range(2):
                        sp.wait_ge(v_added, nb * 2 + (2 * j + i + 1))
                        sp.dma_start(v_buf[i], one(v_rows, nb * 2 + (2 * j + i))).then_inc(v_in[i], 16)
                    for i in range(8):
                        sp.wait_ge(joined_sb, nb * 8 + (8 * j + i + 1))
                        sp.dma_start(adj_buf[i % 4], one(adj_tiles, nb * 8 + (8 * j + i))
                                     ).then_inc(adj_in[i % 4], 16)
            sp.wait_ge(end_sb, 1)
            for i in range(4):
                sp.dma_start(x_buf[i], x_tiles[i]).then_inc(x_in[i], 16)

            def store(t, s):
                sp.wait_ge(fin_sb, t + 1)
                sp.dma_start(one(out_tiles, t), fin_buf[s % 2]).then_inc(stored[s % 2], 16)

            with strided(sp, 0, T - 4, 4) as t:
                for j in range(4):
                    store(t + j, j)
                    sp.dma_start(x_buf[j], one(x_tiles, t + (j + 4))).then_inc(x_in[j], 16)
            for t in range(T - 4, T):
                store(t, t)
            for i in range(2):
                sp.wait_ge(stored[i], 16 * (T // 2) + 16)

        @block.gpsimd
        def _(pool):
            nc.gpsimd.memset(v_acc, 0.0).then_inc(v_added, 2)
            with strided(pool, 0, 2 * NB, 2) as b:
                for j in range(2):
                    pool.wait_ge(v_in[j], b * 8 + 16)
                    pool.wait_ge(v_added, b + (j + 2))
                    nc.gpsimd.tensor_tensor(v_acc, v_acc, v_buf[j], ALU.add).then_inc(v_added, 1)
            pool.wait_ge(lead_ps, 1)
            pool.wait_ge(c_sb, NB + 2)
            pool.wait_ge(joined_sb, HALVES + 4)
            nc.gpsimd.memset(kv_flat, 0.0).then_inc(kv_zeroed, 1)
            nc.gpsimd.memset(O[:, 0:HT, :], 0.0).then_inc(o_zeroed, 1)
            with super_rounds(pool) as r:
                wait_apart(pool, index_ready, r * (2 * CH) + 2 * CH)
                pool.wait_ge(kv_zeroed, 1)

                def gather(t, b, wait):
                    n = r * T + t
                    if wait:
                        wait_apart(pool, prodT_sb, n - (KV - 1))
                    nc.gpsimd.tensor_copy(index_now[:, b, :], index[:, bass.ds(t, 1), :].rearrange("p a c -> p (a c)")
                                          ).then_inc(index_copied, 1)
                    wait_apart(pool, index_copied, n + 1)
                    for c in range(CH):
                        pool.indirect_dma_start(
                            adj_g[:, b, c, :], None, adj_cols,
                            bass.IndirectOffsetOnAxis(index_now[:, b, CH + c:CH + c + 1], 0),
                        ).then_inc(gathered[b], 16)
                    if wait:
                        wait_apart(pool, pv_ps, n - (KV - 1))
                    for c in range(CH):
                        pool.indirect_dma_start(
                            kv[:, b, c, :], None, kv_rows,
                            bass.IndirectOffsetOnAxis(index_now[:, b, c:c + 1], 0),
                            bounds_check=N - 1, oob_is_err=False,
                        ).then_inc(gathered[b], 16)

                for t in range(KV + 2):
                    gather(t, t % KV, t >= KV)
                with strided(pool, KV + 2, T, KV) as t:
                    for j in range(KV):
                        gather(t + j, (KV + 2 + j) % KV, True)
            pool.wait_ge(end_sb, 1)
            with strided(pool, 0, T, 4) as t:
                for j in range(4):
                    pool.wait_ge(x_in[j], t * 4 + 16)
                    nc.gpsimd.tensor_tensor(x_buf[j], x_buf[j], beta[:, :], ALU.add).then_inc(xb_sb, 1)

        @block.tensor
        def _(pe):
            pe.sem_inc(joined_used, 2)
            pe.sem_inc(c_ps, 2)
            pe.wait_ge(cst_in, 16)
            pe.wait_ge(filled, FILLS)
            pe.wait_ge(weights_in, 32)
            for a in range(DC):
                for e in range(DC):
                    mm = nc.tensor.matmul(bank[4 + a][:, :], w_left[:, e, a * P:(a + 1) * P], w_right[:, e, :],
                                          start=(e == 0), stop=(e == DC - 1))
                mm.then_inc(prep_ps, 1)
            bias = [cst[:, C_B + i * DC:C_B + (i + 1) * DC] for i in range(3)]
            for n, (w, b) in enumerate(((w_right, 0), (w_left, 1))):
                for a in range(DC):
                    for e in range(DC):
                        mm = nc.tensor.matmul(bank[2][:, n * DC + a:n * DC + a + 1], w[:, e, a * P:(a + 1) * P],
                                              bias[b][:, e:e + 1], start=(e == 0), stop=(e == DC - 1))
                mm.then_inc(prep_ps, 1)
            nc.tensor.matmul(bank[3][:, 0:DC], ones[:, :], small[:, 0:DC], start=True, stop=True
                             ).then_inc(prep_ps, 1)
            pe.wait_ge(weights2_in, 32)
            pe.wait_ge(prep_sb, DC + 3)
            for a in range(DC):
                for e in range(DC):
                    mm = nc.tensor.matmul(bank[4 + a][:, :], w_left[:, e, a * P:(a + 1) * P], w_right[:, e, :],
                                          start=(e == 0), stop=(e == DC - 1))
                mm.then_inc(prep_ps, 1)
            for e in range(DC):
                mm = nc.tensor.matmul(bank[2][0:1, :], bias[2][:, e:e + 1], w_right[:, e, :],
                                      start=(e == 0), stop=(e == DC - 1))
            mm.then_inc(prep_ps, 1)
            pe.wait_ge(prep_sb, 2 * DC + 4)
            nc.tensor.matmul(bank[3][:, :], ones[0:1, :], beta_row, start=True, stop=True).then_inc(prep_ps, 1)
            pe.wait_ge(prep_sb, 2 * DC + 5)
            for h in range(2):
                nc.tensor.matmul(bank[h][:, 0:P], one_hot[:, P:2 * P], one_hot[:, P:2 * P], start=True, stop=False,
                                 skip_group_check=True)
                with strided(pe, h * NB // 2, (h + 1) * NB // 2, 2) as nb:
                    for j in range(2):
                        pe.wait_ge(xT_in[j], nb * 8 + 16)
                        for a in range(DC):
                            pe.wait_ge(q_sb, nb * DC + (DC * j + a + 1))
                            for d in range(DC):
                                mm = nc.tensor.matmul(bank[2 + a % 2][:, :], M[:, d, a * P:(a + 1) * P],
                                                      xT_buf[j][:, d, :], start=(d == 0), stop=(d == DC - 1))
                            mm.then_inc(q_ps, 1)
                            for hh in range(2):
                                k = 2 * (DC * j + a) + hh
                                wait_apart(pe, joined_sb, nb * 8 + (k + 5))
                                for gg in range(G8 // 2):
                                    m = (DC * j + a) * G8 + hh * (G8 // 2) + gg
                                    at = (127 - m + h * (NB // 2) * DC * G8) - nb * (DC * G8)
                                    mm = nc.tensor.matmul(bank[h][:, :], cols(one_hot, at, P),
                                                          joined[hh][:, gg * GK:(gg + 1) * GK],
                                                          start=False, stop=False, skip_group_check=True)
                                mm.then_inc(joined_used, 1)
                        pe.wait_ge(c_sb, nb + (j + 1))
                        for k in range(4):
                            for d in range(DC):
                                mm = nc.tensor.matmul(bank[4 + j][:, k:k + 1],
                                                      xT_buf[j][:, d, k * P:(k + 1) * P], w_col[:, d:d + 1],
                                                      start=(d == 0), stop=(d == DC - 1))
                        mm.then_inc(c_ps, 1)
            pe.wait_ge(v_added, 2 + 2 * NB)
            pe.wait_ge(c_sb, NB + 2)
            for k in range(2):
                mm = nc.tensor.matmul(bank[2][:, :], ones[:, :], v_acc[:, k * D:(k + 1) * D],
                                      start=(k == 0), stop=(k == 1))
            mm.then_inc(lead_ps, 1)
            nc.tensor.transpose(bank[3][0:T, 0:P], c_cols[:, :], ident).then_inc(lead_ps, 1)
            pe.wait_ge(lead_sb, 5)
            nc.tensor.matmul(bank[4][0:1, 0:P], small[:, 42:43], ident, start=True, stop=True).then_inc(lead_ps, 1)

            with super_rounds(pe) as r:
                for k in range(2 * CH):
                    pe.wait_ge(spread_sb, r * (2 * CH) + (k + 1))
                    mm = nc.tensor.matmul(bank[5][:, k * HT:(k + 1) * HT],
                                          spread[k % 2].rearrange("p g s -> p (g s)"), tile_select,
                                          start=True, stop=True)
                    mm.then_inc(spread_ps, 1)
                wait_apart(pe, index_ready, r * (2 * CH) + 2 * CH)

                def step(t, third, s, new, mid, old):
                    n, p = r * T + t, s % 2

                    def keys(c):
                        if not (s < 1 and c < 2):
                            pe.wait_ge(keyT_sb, n * CH + (c - 1))
                        ps = bank[4 + (s * CH + c) % 2]
                        for a in range(DC):
                            mm = nc.tensor.transpose(ps[:, a * P:(a + 1) * P], kv[:, s % KV, c, a * P:(a + 1) * P],
                                                     ident)
                        mm.then_inc(keyT_ps, 1)

                    def scores(c):
                        pe.wait_ge(keyT_sb, n * CH + (c + 1))
                        ps = bank[6 + p][:, c * P:(c + 1) * P]
                        for a in range(DC):
                            mm = nc.tensor.matmul(ps, keyT[:, c, a * P:(a + 1) * P], cols(qT[:, a, :], t * P, P),
                                                  start=False, stop=(a == DC - 1), skip_group_check=True)
                        return mm

                    def values(c):
                        return nc.tensor.matmul(bank[2 + p][:, :], probT[:, p, c * P:(c + 1) * P],
                                                kv[:, (s - 2) % KV, c, D:2 * D], start=(c == 0), stop=(c == CH - 1))

                    if old:
                        pe.wait_ge(probT_sb, n - 1)
                        if s >= 4:
                            pe.wait_ge(o_sb, n - 3)
                        for c in range(CH - 1):
                            values(c)
                    if mid:
                        pe.wait_ge(prodT_sb, n)
                        if s >= 2:
                            pe.wait_ge(masked, n - 1)
                        for c in range(CH):
                            mm = nc.tensor.transpose(bank[0][:, c * P:(c + 1) * P],
                                                     prodT[:, 1 - p, c * P:(c + 1) * P], ident)
                        mm.then_inc(prod_ps, 1)
                    if old:
                        values(CH - 1).then_inc(pv_ps, 1)
                    if new:
                        pe.wait_ge(gathered[s % KV], (r * IN_BUF[s % KV] + (third + 1)) * (32 * CH))
                        keys(0)
                        keys(1)
                    if new:
                        pe.wait_ge(c_ready, n + 1)
                        if s >= 2:
                            pe.wait_ge(prodT_sb, n - 1)
                        nc.tensor.matmul(bank[6 + p][:, 0:SLOTS], ones[:, :],
                                         c_diag[:, p, :].unsqueeze(1).broadcast_to([P, CH, P]),
                                         start=True, stop=False, skip_group_check=True)
                        scores(0)
                        keys(2)
                        scores(1)
                    if mid:
                        pe.wait_ge(weight_sb, n)
                        if s >= 2:
                            pe.wait_ge(probT_sb, n - 1)
                        for c in range(CH):
                            mm = nc.tensor.transpose(bank[1][:, c * P:(c + 1) * P], prob[:, c * P:(c + 1) * P], ident)
                        mm.then_inc(probT_ps, 1)
                    if new:
                        scores(2).then_inc(score_ps, 1)

                tile_steps(pe, step)

            def out_step(t, s, new, old):
                if new:
                    pe.wait_ge(on_sb, t + 1)
                    if s >= 2:
                        pe.wait_ge(onT_sb, t - 1)
                    for a in range(DC):
                        mm = nc.tensor.transpose(bank[4 + s % 2][:, a * P:(a + 1) * P],
                                                 on_buf[s % 2][:, a * P:(a + 1) * P], ident)
                    mm.then_inc(onT_ps, 1)
                if old:
                    pe.wait_ge(onT_sb, t)
                    if s >= 3:
                        pe.wait_ge(y_sb, t - 2)
                    for a in range(DC):
                        mm = nc.tensor.matmul(bank[6 + s % 2][:, :], onT_buf[(s - 1) % 2][:, a, :], G[:, a, :],
                                              start=(a == 0), stop=(a == DC - 1))
                    mm.then_inc(y_ps, 1)

            for t in range(4):
                out_step(t, t, True, t >= 1)
            with strided(pe, 4, T, 4) as t:
                for j in range(4):
                    out_step(t + j, 4 + j, True, True)
            out_step(T, 4, False, True)

        @block.scalar
        def _(act):
            act.sem_inc(q_sb, 2)
            act.sem_inc(c_sb, 2)
            act.wait_ge(prep_ps, DC + 2)
            act.dma_start(w_left, wv.rearrange("(e p) d -> p e d", p=P)).then_inc(weights2_in, 16)
            act.dma_start(w_right, wmT.rearrange("(e p) d -> p e d", p=P)).then_inc(weights2_in, 16)
            act.wait_ge(prep_sb, DC + 3)
            with strided(act, 0, NB, 2) as nb:
                for j in range(2):
                    for a in range(DC):
                        act.wait_ge(q_ps, nb * DC + (DC * j + a + 1))
                        nc.scalar.activation(cols(qT[:, a, :], nb * 512 + 512 * j, 512), bank[2 + a % 2][:, :],
                                             ACT.Identity, bias=u_col[:, a:a + 1]).then_inc(q_sb, 1)
                    act.wait_ge(c_ps, nb + (j + 3))
                    nc.scalar.activation(cols(c_cols, nb * 4 + 4 * j, 4), bank[4 + j][:, 0:4],
                                         ACT.Identity, bias=kappa).then_inc(c_sb, 1)
            act.wait_ge(lead_ps, 1)
            with act.Fori(HT, T) as t:
                nc.scalar.activation(O[:, bass.ds(t, 1), :].rearrange("p a d -> p (a d)"), zero_row, ACT.Copy
                                     ).then_inc(o_zeroed, 1)

            with super_rounds(act) as r:
                act.wait_ge(index_ready, r * (2 * CH) + 2 * CH)

                def size_of_scores(n):
                    act.wait_ge(prod_ps, n)
                    nc.scalar.activation(is_tiny[:, :], bank[0][:, 0:SLOTS], ACT.Abs).then_inc(abs_sb, 1)

                def step(t, third, s, new, mid, old):
                    n, p = r * T + t, s % 2

                    def copy_keys(c):
                        act.wait_ge(keyT_ps, n * CH + (c + 1))
                        if s >= 1:
                            act.wait_ge(score_ps, n)
                        nc.scalar.activation(keyT[:, c, :], bank[4 + (s * CH + c) % 2][:, :], ACT.Copy
                                             ).then_inc(keyT_sb, 1)

                    if mid:
                        size_of_scores(n)
                    if new:
                        copy_keys(0)
                        copy_keys(1)
                    if mid:
                        q = 1 - p
                        act.wait_ge(new_max_sb, n)
                        nc.scalar.activation(alpha[:, q:q + 1], cols(neg_max, t - 1, 1), ACT.Exp,
                                             bias=new_max[:, q:q + 1], scale=-1.0).then_inc(exp_sb, 1)
                        nc.scalar.activation(p_rest[:, q:q + 1], cst[:, C_NEG:C_NEG + 1], ACT.Exp,
                                             bias=new_max[:, q:q + 1]).then_inc(exp_sb, 1)
                        nc.scalar.activation(prob[:, :], score[:, :], ACT.Exp, bias=new_max[:, q:q + 1],
                                             accum_out=p_sum[:, q:q + 1]).then_inc(exp_sb, 1)
                    if new:
                        copy_keys(2)
                    if mid:
                        act.wait_ge(probT_ps, n)
                        if s >= 3:
                            act.wait_ge(pv_ps, n - 2)
                        nc.scalar.activation(probT[:, q, :], bank[1][:, 0:SLOTS], ACT.Copy).then_inc(probT_sb, 1)

                tile_steps(act, step)
            act.wait_ge(rest_sb, 1)
            nc.scalar.activation(p_all, neg_max[:, :], ACT.Exp, bias=cst[:, C_NEG:C_NEG + 1]).then_inc(end_exp, 1)

            def out_step(t, s, new, old):
                if new:
                    act.wait_ge(onT_ps, t + 1)
                    if s >= 2:
                        act.wait_ge(y_ps, t - 1)
                    nc.scalar.activation(onT_buf[s % 2].rearrange("p a r -> p (a r)"), bank[4 + s % 2][:, :], ACT.Copy
                                         ).then_inc(onT_sb, 1)
                if old:
                    act.wait_ge(mean_sb, t - 1)
                    nc.scalar.activation(std[:, s % 2:s % 2 + 1], mean_var[:, s % 2, 1:2], ACT.Sqrt,
                                         bias=cst[:, C_EPS:C_EPS + 1]).then_inc(std_sb, 1)

            for t in range(4):
                out_step(t, t, True, t >= 2)
            with strided(act, 4, T, 4) as t:
                for j in range(4):
                    out_step(t + j, 4 + j, True, True)
            out_step(T, 4, False, True)
            out_step(T + 1, 5, False, True)

        @block.vector
        def _(dve):
            dve.sem_inc(joined_sb, 4)
            dve.sem_inc(stored[0], 16)
            dve.sem_inc(stored[1], 16)
            nc.vector.memset(ones[:, :], 1.0).then_inc(filled, 1)
            nc.vector.memset(zero_row, 0.0).then_inc(filled, 1)
            nc.vector.memset(c_rows[:, :], 0.0).then_inc(filled, 1)
            nc.vector.memset(neg_max[:, :], -MASKED).then_inc(filled, 1)
            nc.vector.memset(denom[:, :], 0.0).then_inc(filled, 1)
            nc.vector.memset(one_hot, 0.0).then_inc(filled, 1)
            nc.vector.memset(kappa, 0.0).then_inc(filled, 1)
            dve.wait_ge(filled, 7)
            nc.vector.memset(one_hot[:, 127:128], 1.0).then_inc(filled, 1)
            dve.wait_ge(cst_in, 16)
            nc.vector.tensor_tensor(small[:, 0:DC], cst[:, C_B:C_B + DC], cst[:, C_B + DC:C_B + 2 * DC], ALU.mult
                                    ).then_inc(filled, 1)
            for a in range(DC):
                dve.wait_ge(prep_ps, a + 1)
                nc.vector.tensor_scalar(M[:, a, :], bank[4 + a][:, :], INV_SCALE, None, ALU.mult).then_inc(prep_sb, 1)
            dve.wait_ge(prep_ps, DC + 2)
            nc.vector.tensor_scalar(u_col, bank[2][:, 0:DC], INV_SCALE, None, ALU.mult).then_inc(prep_sb, 1)
            nc.vector.tensor_scalar(w_col, bank[2][:, DC:2 * DC], INV_SCALE, None, ALU.mult).then_inc(prep_sb, 1)
            dve.wait_ge(prep_ps, DC + 3)
            nc.vector.tensor_scalar(small[:, 8:8 + DC], bank[3][:, 0:DC], INV_SCALE, 0.0, ALU.mult, ALU.add,
                                    accum_out=kappa).then_inc(prep_sb, 1)
            for a in range(DC):
                dve.wait_ge(prep_ps, DC + 4 + a)
                nc.vector.tensor_copy(G[:, a, :], bank[4 + a][:, :]).then_inc(prep_sb, 1)
            dve.wait_ge(prep_ps, 2 * DC + 4)
            dve.wait_ge(bm_in, 16)
            nc.vector.tensor_tensor(beta_row, bank[2][0:1, :], bm_row, ALU.add).then_inc(prep_sb, 1)
            dve.wait_ge(prep_ps, 2 * DC + 5)
            nc.vector.tensor_copy(beta[:, :], bank[3][:, :]).then_inc(prep_sb, 1)
            with dve.Fori(0, HALVES // 4) as k:
                for i in range(4):
                    dve.wait_ge(adj_in[i], k * 16 + 16)
                    dve.wait_ge(joined_used, k * 4 + (i + 1))
                    nc.vector.tensor_scalar(joined[i % 2], adj_buf[i], 0.0, None, ALU.not_equal
                                            ).then_inc(joined_sb, 1)
            dve.wait_ge(joined_used, HALVES + 2)
            for h in range(2):
                nc.vector.scalar_tensor_tensor(left[:, h, :], bank[h][:, :], 0.0, descending, ALU.is_gt, ALU.mult
                                               ).then_inc(lead_sb, 1)
            dve.wait_ge(lead_sb, 2)
            for h in range(2):
                nc.vector.tensor_scalar(keyT[:, h, :], left[:, h, :], 0.0, 0.0, ALU.is_gt, ALU.add,
                                        accum_out=small[:, 40 + h:41 + h]).then_inc(lead_sb, 1)
            dve.wait_ge(lead_sb, 4)
            nc.vector.tensor_tensor(small[:, 42:43], small[:, 40:41], small[:, 41:42], ALU.max).then_inc(lead_sb, 1)
            dve.wait_ge(lead_ps, 1)
            nc.vector.tensor_copy(vsum[:, :], bank[2][:, :]).then_inc(lead_sb, 1)
            dve.wait_ge(lead_ps, 2)
            nc.vector.tensor_copy(c_rows[0:T, :], bank[3][0:T, 0:P]).then_inc(lead_sb, 1)
            dve.wait_ge(lead_ps, 3)
            nc.vector.tensor_reduce(small[0:1, 43:44], bank[4][0:1, 0:P], AX_X, ALU.max).then_inc(lead_sb, 1)
            dve.wait_ge(lead_sb, 8)
            nc.vector.tensor_scalar(small[0:1, 44:44 + MAXR], cst[0:1, C_THR:C_THR + MAXR], small[0:1, 43:44], 0.0,
                                    ALU.is_lt, ALU.add, accum_out=small[0:1, 60:61]).then_inc(lead_sb, 1)
            dve.wait_ge(lead_sb, 9)
            nc.vector.tensor_copy(rounds_i[:, :], small[0:1, 60:61]).then_inc(rounds_ready, 1)

            with super_rounds(dve) as r:
                k = 0
                for h in range(2):
                    for i in range(0, GS, 8):
                        if k:
                            wait_apart(dve, took, r * TAKES + k)
                        nc.vector.max(slots[:, h, i:i + 8], left[:, h, :]).then_inc(took, 1)
                        wait_apart(dve, took, r * TAKES + (k + 1))
                        nc.vector.match_replace(left[:, h, :], slots[:, h, i:i + 8], left[:, h, :], 0.0
                                                ).then_inc(took, 1)
                        k += 2
                for c in range(CH):
                    for h in range(2):
                        k = 2 * c + h
                        if k >= 2:
                            dve.wait_ge(spread_ps, r * (2 * CH) + (k - 1))
                        nc.vector.tensor_tensor(spread[k % 2], group_mask,
                                                slots[:, h, c * SPC:(c + 1) * SPC].unsqueeze(1)
                                                .broadcast_to([P, G8, SPC]), ALU.mult).then_inc(spread_sb, 1)
                dve.wait_ge(spread_ps, r * (2 * CH) + 2 * CH)
                for c in range(CH):
                    v = bank[5][:, c * T:(c + 1) * T]
                    nc.vector.tensor_scalar(index[:, :, c], v, -float(G8), cst[:, C_BK:C_BK + 1], ALU.mult, ALU.add
                                            ).then_inc(index_ready, 1)
                    nc.vector.scalar_tensor_tensor(index[:, :, CH + c], v, -float(G8 * T), cst[:, C_BA:C_BA + T],
                                                   ALU.mult, ALU.add).then_inc(index_ready, 1)
                dve.wait_ge(o_zeroed, 1 + HT)

                def step(t, third, s, new, mid, old):
                    n, p = r * T + t, s % 2
                    if new:
                        nc.vector.tensor_scalar(c_diag[:, p, :], c_rows[:, :], cols(ident, t, 1), None, ALU.mult
                                                ).then_inc(c_ready, 1)
                    if mid:
                        q = 1 - p
                        dve.wait_ge(prod_ps, n)
                        prod = bank[0][:, 0:SLOTS]
                        dve.wait_ge(abs_sb, n)
                        nc.vector.tensor_scalar(is_tiny[:, :], is_tiny[:, :], TINY, MASKED, ALU.is_lt, ALU.mult
                                                ).then_inc(tiny_sb, 1)
                        dve.wait_ge(tiny_sb, n)
                        nc.vector.tensor_tensor(score[:, :], is_tiny[:, :], prod, ALU.add).then_inc(masked, 1)
                        dve.wait_ge(masked, n)
                        nc.vector.tensor_reduce(chunk_max[:, q:q + 1], score[:, :], AX_X, ALU.max, negate=True
                                                ).then_inc(max_sb, 1)
                        dve.wait_ge(max_sb, n)
                        nc.vector.tensor_tensor(new_max[:, q:q + 1], chunk_max[:, q:q + 1], cols(neg_max, t - 1, 1),
                                                ALU.min).then_inc(new_max_sb, 1)
                    if old:
                        dve.wait_ge(pv_ps, n - 1)
                        acc = O[:, bass.ds(t - 2, 1), :].rearrange("p a d -> p (a d)")
                        nc.vector.scalar_tensor_tensor(acc, acc, alpha[:, p:p + 1], bank[2 + p][:, :],
                                                       ALU.mult, ALU.add).then_inc(o_sb, 1)
                    if mid:
                        dve.wait_ge(exp_sb, n * 3)
                        nc.vector.tensor_scalar(prob[:, :], prob[:, :], p_rest[:, q:q + 1], None, ALU.subtract
                                                ).then_inc(weight_sb, 1)
                        nc.vector.scalar_tensor_tensor(l_add[:, q:q + 1], p_rest[:, q:q + 1], -float(SLOTS),
                                                       p_sum[:, q:q + 1], ALU.mult, ALU.add).then_inc(sum_sb, 1)
                        dve.wait_ge(sum_sb, n)
                        l = cols(denom, t - 1, 1)
                        nc.vector.scalar_tensor_tensor(l, l, alpha[:, q:q + 1], l_add[:, q:q + 1],
                                                       ALU.mult, ALU.add).then_inc(state_sb, 1)
                        nc.vector.tensor_copy(cols(neg_max, t - 1, 1), new_max[:, q:q + 1]).then_inc(state_sb, 1)
                    if new:
                        dve.wait_ge(score_ps, n + 1)
                        nc.vector.tensor_tensor(prodT[:, p, :], bank[6 + p][:, 0:SLOTS],
                                                adj_g[:, s % KV, :, :].rearrange("p c r -> p (c r)"), ALU.mult
                                                ).then_inc(prodT_sb, 1)

                tile_steps(dve, step)
                dve.wait_ge(o_sb, r * T + T)
                dve.wait_ge(state_sb, r * (2 * T) + 2 * T)
            dve.sem_inc(rest_sb, 1)
            dve.sem_inc(end_sb, 1)
            dve.wait_ge(end_exp, 1)
            nc.vector.scalar_tensor_tensor(denom[:, :], p_all, float(N), denom[:, :], ALU.mult, ALU.add
                                           ).then_inc(end_l, 1)
            dve.wait_ge(end_l, 1)
            nc.vector.reciprocal(r_denom[:, :], denom[:, :]).then_inc(end_l, 1)
            dve.wait_ge(end_l, 2)

            def out_step(t, s, new, mid, old):
                if new:
                    if s >= 2:
                        dve.wait_ge(onT_ps, t - 1)
                    nc.vector.scalar_tensor_tensor(on_buf[s % 2], vsum[:, :], cols(p_all, t, 1),
                                                   O[:, bass.ds(t, 1), :].rearrange("p a d -> p (a d)"),
                                                   ALU.mult, ALU.add).then_inc(on_sb, 1)
                if mid:
                    b = s % 2
                    dve.wait_ge(y_ps, t - 1)
                    dve.wait_ge(xb_sb, t - 1)
                    if s >= 4:
                        dve.wait_ge(fin_sb, t - 3)
                    nc.vector.scalar_tensor_tensor(y_buf[b], bank[6 + (s + 1) % 2][:, :], cols(r_denom, t - 2, 1),
                                                   x_buf[(s - 2) % 4], ALU.mult, ALU.add).then_inc(y_sb, 1)
                    dve.wait_ge(y_sb, t - 1)
                    nc.vector.bn_stats(stats[:, b, :], y_buf[b]).then_inc(stats_sb, 1)
                    wait_apart(dve, stats_sb, t - 1)
                    nc.vector.bn_aggr(mean_var[:, b, :], stats[:, b, :]).then_inc(mean_sb, 1)
                if old:
                    b = (s - 3) % 2
                    dve.wait_ge(std_sb, t - 2)
                    nc.vector.reciprocal(rstd[:, b:b + 1], std[:, b:b + 1]).then_inc(rstd_sb, 1)
                    dve.wait_ge(rstd_sb, t - 2)
                    dve.wait_ge(stored[b], (t - s) * 8 + (16 * ((s - 3) // 2) + 16))
                    nc.vector.tensor_scalar(fin_buf[b], y_buf[b], mean_var[:, b, 0:1], rstd[:, b:b + 1],
                                            ALU.subtract, ALU.mult).then_inc(fin_sb, 1)

            for t in range(4):
                out_step(t, t, True, t >= 2, t >= 3)
            with strided(dve, 4, T, 4) as t:
                for j in range(4):
                    out_step(t + j, 4 + j, True, True, True)
            for t in range(T, T + 3):
                out_step(t, t, False, t < T + 2, True)


def layout(adj, key, value, x, Wq, Wk, Wv, Wm, bq, bk, bv, bm):
    import numpy as np

    a = adj.reshape(P, T, GK, 2, G8 // 2)
    const = np.zeros((P, C_ALL), np.float32)
    p = np.arange(P)
    const[:, C_ID:C_ID + P] = np.eye(P)
    const[:, C_DESC:C_DESC + GK] = GK - np.arange(GK)
    const[:, C_GRP:C_GRP + P] = (p % G8)[:, None] == (p // SPC)[None, :]
    const[:, C_SEL:C_SEL + HT] = (p // G8)[:, None] == np.arange(HT)[None, :]
    const[:, C_BK] = N + p // SPC
    const[:, C_BA:C_BA + T] = (T * (N + p // SPC))[:, None] + np.arange(T)[None, :]
    const[:, C_THR:C_THR + MAXR] = np.array([-1] + [GS * q for q in range(1, MAXR)])
    const[:, C_NEG] = MASKED
    const[:, C_EPS] = 1e-5
    for i, b in enumerate((bq, bk, bv)):
        const[:, C_B + i * DC:C_B + (i + 1) * DC] = b.reshape(DC, P).T
    return {
        "adj_tiles": np.ascontiguousarray(a.transpose(1, 3, 0, 4, 2)).reshape(HALVES, P, N // 2),
        "adj_cols": np.concatenate([adj.reshape(P, T, N).transpose(2, 1, 0).reshape(N * T, P),
                                    np.zeros((G8 * T, P), adj.dtype)]),
        "kv_rows": np.concatenate([key, value], axis=1),
        "value": value,
        "x": x,
        "xT": np.ascontiguousarray(x.reshape(P, NB, T // NB, DC, P).transpose(1, 4, 3, 2, 0)).reshape(NB, P, DC, 512),
        "wq": Wq, "wk": Wk, "wv": Wv, "wmT": np.ascontiguousarray(Wm.T),
        "bm": bm.reshape(1, D),
        "consts": const,
    }


def kernel(x, adj, L0_gnn_key, L0_gnn_value, L0_gnn_Wq, L0_gnn_bq, L0_gnn_Wk, L0_gnn_bk, L0_gnn_Wv, L0_gnn_bv,
           L0_gnn_Wm, L0_gnn_bm):
    import numpy as np
    import concourse.bacc as bacc
    from concourse.bass_utils import run_bass_kernel_spmd

    given = [np.asarray(i) for i in (adj, L0_gnn_key, L0_gnn_value, x, L0_gnn_Wq, L0_gnn_Wk, L0_gnn_Wv, L0_gnn_Wm,
                                     L0_gnn_bq, L0_gnn_bk, L0_gnn_bv, L0_gnn_bm)]
    arrays = layout(*given)
    nc = bacc.Bacc("TRN2", target_bir_lowering=False, num_devices=1)
    args = {n: nc.dram_tensor(n, a.shape, mybir.dt.from_np(a.dtype), kind="ExternalInput").ap()
            for n, a in arrays.items()}
    out = nc.dram_tensor("out", (N, D), F32, kind="ExternalOutput").ap()
    build(nc, out=out, **args)
    r = run_bass_kernel_spmd(nc, [arrays], core_ids=[0])
    return r.results[0]["out"]
```

```python
from contextlib import ExitStack, contextmanager

import concourse.bass as bass
from concourse import mybir

F32 = mybir.dt.float32
BF16 = mybir.dt.bfloat16
I32 = mybir.dt.int32
ALU = mybir.AluOpType
ACT = mybir.ActivationFunctionType
AX_X = mybir.AxisListType.X

P = 128
N = 4096
D = 512
DC = D // P
T = N // P
HT = T // 2
G8 = P // HT
GK = N // G8
CH = 3
SLOTS = CH * P
GS = SLOTS // G8
SPC = P // G8
MAXR = -(-GK // GS)
NB = N // 512
HALVES = 2 * T
KV = 3
INV_SCALE = 1.0 / float(N) ** 0.5
MASKED = -1e9
TINY = 1e-5

C_ID = 0
C_DESC = C_ID + P
C_GRP = C_DESC + GK
C_SEL = C_GRP + P
C_BK = C_SEL + HT
C_BA = C_BK + 1
C_THR = C_BA + T
C_NEG = C_THR + MAXR - 1
C_EPS = C_NEG + 1
C_CUT = C_EPS + 1
C_B = C_CUT + T
C_ALL = C_B + 3 * DC


@contextmanager
def strided(eng, start, stop, step):
    with eng.Fori(0, (stop - start) // step) as m:
        yield m * step + start


def build(nc, adj_tiles, adj_cols, kv_rows, value, x, xT, wq, wk, wv, wmT, bm, consts, out):
    with ExitStack() as ctx:
        def sb(name, shape, dt=F32):
            return ctx.enter_context(nc.sbuf_tensor(name, shape, dt))

        def sem(name):
            return ctx.enter_context(nc.semaphore(name))

        bank = [ctx.enter_context(nc.psum_tensor(f"bank{i}", [P, 512], F32)) for i in range(8)]

        cst = sb("cst", [P, C_ALL])
        ident = cst[:, C_ID:C_ID + P]
        descending = cst[:, C_DESC:C_DESC + GK]
        group_mask = cst[:, C_GRP:C_GRP + P].rearrange("p (g s) -> p g s", g=G8)
        cut_select = cst[0:3 * T, C_CUT:C_CUT + T]
        tile_select = cst[:, C_SEL:C_SEL + HT]
        qT = sb("qT", [P, DC, N])
        G = sb("G", [P, DC, D])
        beta = sb("beta", [P, D])
        vsum = sb("vsum", [P, D])
        ones = sb("ones", [P, P])
        left = sb("left", [P, 2, GK])
        c_cols = sb("c_cols", [P, T])
        c_cuts = sb("c_cuts", [P, 3, T])
        c_cut = sb("c_cut", [P, T], BF16)
        c_rows = sb("c_rows", [3 * T, P], BF16)
        ones_bf = sb("ones_bf", [3 * T, P], BF16)
        slots = sb("slots", [P, 2, GS])
        index = sb("index", [P, T, 2 * CH], I32)
        neg_max = sb("neg_max", [P, T])
        denom = sb("denom", [P, T])
        small = sb("small", [P, 64])
        rounds_i = sb("rounds_i", [1, 1], I32)

        O = sb("O", [P, T, D])
        o_flat = O[:, :, :].rearrange("p t d -> p (t d)")
        adj_buf = [o_flat[:, i * 2048:(i + 1) * 2048] for i in range(4)]
        joined = [o_flat[:, 8192 + i * 1024:8192 + (i + 1) * 1024].bitcast(BF16) for i in range(2)]
        xT_buf = [o_flat[:, 10240 + i * 2048:10240 + (i + 1) * 2048].rearrange("p (d n) -> p d n", d=DC)
                  for i in range(2)]
        v_buf = [o_flat[:, 14336 + i * 1024:14336 + (i + 1) * 1024] for i in range(2)]

        kv = sb("kv", [P, KV, CH, 2 * D])
        kv_flat = kv[:, :, :, :].rearrange("p b c d -> p (b c d)")
        w_left = kv_flat[:, 0:2048].rearrange("p (e d) -> p e d", e=DC)
        w_right = kv_flat[:, 2048:4096].rearrange("p (e d) -> p e d", e=DC)
        v_left = kv_flat[:, 5120:7168].rearrange("p (e d) -> p e d", e=DC)
        m_right = kv_flat[:, 7168:9216].rearrange("p (e d) -> p e d", e=DC)
        beta_row = kv_flat[0:1, 4096:4096 + D]
        bm_row = kv_flat[0:1, 4608:4608 + D]

        adj_g = sb("adj_g", [P, KV, CH, P])
        keyT = sb("keyT", [P, CH, D])
        v_acc = keyT[:, 0:2, :].rearrange("p c d -> p (c d)")
        c_part = keyT[:, 2, :]
        work = sb("work", [P, 2064])
        prodT = work[:, 0:2 * SLOTS].rearrange("p (b s) -> p b s", b=2)
        probT = work[:, 2 * SLOTS:4 * SLOTS].rearrange("p (b s) -> p b s", b=2)
        score = work[:, 4 * SLOTS:5 * SLOTS]
        M = work[:, 0:DC * D].rearrange("p (a d) -> p a d", a=DC)
        u_col = work[:, 2048:2052]
        w_col = work[:, 2052:2056]
        kappa = work[:, 2056:2057]
        c_tile = sb("c_tile", [P, 2, P], BF16)
        one_hot = c_tile[:, :, :].rearrange("p b r -> p (b r)")
        index_now = sb("index_now", [P, KV, 2 * CH], I32)
        chunk_max = sb("chunk_max", [P, 2])
        new_max = sb("new_max", [P, 2])
        alpha = sb("alpha", [P, 2])
        p_rest = sb("p_rest", [P, 2])
        p_sum = sb("p_sum", [P, 2])
        l_add = sb("l_add", [P, 2])
        spread = sb("spread", [P, CH, G8, SPC])

        x_buf = [kv_flat[:, i * 512:(i + 1) * 512] for i in range(4)]
        on_buf = [kv_flat[:, 3072 + i * 512:3072 + (i + 1) * 512] for i in range(2)]
        onT_buf = [kv_flat[:, 4096 + i * 512:4096 + (i + 1) * 512].rearrange("p (a r) -> p a r", a=DC)
                   for i in range(2)]
        y_buf = [kv_flat[:, 5120 + i * 512:5120 + (i + 1) * 512] for i in range(2)]
        fin_buf = [kv_flat[:, 6144 + i * 512:6144 + (i + 1) * 512] for i in range(2)]
        stats = kv_flat[:, 7168:7180].rearrange("p (b s) -> p b s", b=2)
        mean_var = kv_flat[:, 7184:7188].rearrange("p (b s) -> p b s", b=2)
        std = kv_flat[:, 7192:7194]
        rstd = kv_flat[:, 7200:7202]
        p_all = small[:, 0:T]
        r_denom = denom


        cst_in = sem("cst_in")
        passed = sem("passed")
        weights_in = sem("weights_in")
        weights2_in = sem("weights2_in")
        bm_in = sem("bm_in")
        filled = sem("filled")
        prep_ps = sem("prep_ps")
        prep_sb = sem("prep_sb")
        adj_in = [sem(f"adj_in{i}") for i in range(4)]
        xT_in = [sem(f"xT_in{i}") for i in range(2)]
        v_in = [sem(f"v_in{i}") for i in range(2)]
        v_added = sem("v_added")
        joined_sb = sem("joined_sb")
        joined_used = sem("joined_used")
        q_ps = sem("q_ps")
        q_sb = sem("q_sb")
        c_part_sb = sem("c_part_sb")
        c_ps = sem("c_ps")
        c_sb = sem("c_sb")
        left_sb = sem("left_sb")
        lead_sb = sem("lead_sb")
        lead_ps = sem("lead_ps")
        kv_zeroed = sem("kv_zeroed")
        rounds_ready = sem("rounds_ready")
        took = sem("took")
        cuts_sb = sem("cuts_sb")
        spread_sb = sem("spread_sb")
        spread_ps = sem("spread_ps")
        index_ready = sem("index_ready")
        index_copied = sem("index_copied")
        gathered = [sem(f"gathered{i}") for i in range(KV)]
        keyT_ps = sem("keyT_ps")
        keyT_sb = sem("keyT_sb")
        c_ready = sem("c_ready")
        score_ps = sem("score_ps")
        prodT_sb = sem("prodT_sb")
        prod_ps = sem("prod_ps")
        abs_sb = sem("abs_sb")
        tiny_sb = sem("tiny_sb")
        masked = sem("masked")
        max_sb = sem("max_sb")
        new_max_sb = sem("new_max_sb")
        alpha_sb = sem("alpha_sb")
        exp_sb = sem("exp_sb")
        weight_sb = sem("weight_sb")
        sum_sb = sem("sum_sb")
        denom_sb = sem("denom_sb")
        state_sb = sem("state_sb")
        probT_ps = sem("probT_ps")
        probT_sb = sem("probT_sb")
        pv_ps = sem("pv_ps")
        o_sb = sem("o_sb")
        rest_sb = sem("rest_sb")
        end_sb = sem("end_sb")
        end_exp = sem("end_exp")
        end_l = sem("end_l")
        x_in = [sem(f"x_in{i}") for i in range(4)]
        xb_sb = sem("xb_sb")
        on_sb = sem("on_sb")
        onT_ps = sem("onT_ps")
        onT_sb = sem("onT_sb")
        y_ps = sem("y_ps")
        y_sb = sem("y_sb")
        stats_sb = sem("stats_sb")
        mean_sb = sem("mean_sb")
        std_sb = sem("std_sb")
        rstd_sb = sem("rstd_sb")
        fin_sb = sem("fin_sb")
        stored = [sem(f"stored{i}") for i in range(2)]

        FILLS = 5
        TAKES = 4 * GS // 8
        x_tiles = x.rearrange("(r t) d -> t r d", t=T)
        out_tiles = out.rearrange("(r t) d -> t r d", t=T)
        v_rows = value.rearrange("(b p k) d -> b p (k d)", p=P, k=2)

        def one(ap, i):
            return ap[bass.ds(i, 1)].rearrange("a p n -> p (a n)")

        def cols(ap, start, n):
            return ap[:, bass.ds(start, n)]

        def wait_apart(eng, s, value):
            eng.wait_ge(s, value)
            eng.sem_inc(passed, 1)

        def tile_steps(eng, step):
            step(0, 0, 0, True, False, False)
            step(1, 0, 1, True, True, False)
            with eng.Fori(0, (T - 2) // 6) as m:
                for j in range(6):
                    step(m * 6 + (2 + j), m * 2 + (2 + j) // KV, 2 + j, True, True, True)
            step(T, T // KV, T % 6, False, True, True)
            step(T + 1, (T + 1) // KV, (T + 1) % 6, False, False, True)

        @contextmanager
        def more_rounds(eng):
            eng.wait_ge(rounds_ready, 1)
            n = eng.value_load(rounds_i[0:1, 0:1], min_val=0, max_val=MAXR - 1)
            with eng.If(n > 0):
                with eng.Fori(0, n) as m:
                    yield m + 1

        IN_BUF = [len(range(b, T, KV)) for b in range(KV)]

        block = ctx.enter_context(nc.Block())

        @block.sync
        def _(sp):
            sp.dma_start(cst[:, :], consts).then_inc(cst_in, 16)
            sp.dma_start(w_left, wq.rearrange("(e p) d -> p e d", p=P)).then_inc(weights_in, 16)
            sp.dma_start(w_right, wk.rearrange("(e p) d -> p e d", p=P)).then_inc(weights_in, 16)
            sp.dma_start(bm_row, bm).then_inc(bm_in, 16)
            def load_values(b, i):
                sp.wait_ge(v_added, b + 1)
                sp.dma_start(v_buf[i], one(v_rows, b)).then_inc(v_in[i], 16)

            def load_xT(nb, j):
                sp.wait_ge(c_ps, nb + 1)
                sp.dma_start(xT_buf[j], xT[bass.ds(nb, 1)].rearrange("a p d n -> p (a d) n")
                             ).then_inc(xT_in[j], 16)

            def load_block(nb, j, first=False):
                for i in range(8):
                    sp.wait_ge(joined_sb, nb * 8 + (i + 1))
                    sp.dma_start(adj_buf[i % 4], one(adj_tiles, nb * 8 + i)).then_inc(adj_in[i % 4], 16)
                    if i == 1:
                        for k in range(2):
                            load_values(nb * 2 + k, k)
                    if i == 3:
                        load_xT(nb, j)
                    if i == 5 and first:
                        sp.dma_start(v_left, wv.rearrange("(e p) d -> p e d", p=P)).then_inc(weights2_in, 16)
                        sp.dma_start(m_right, wmT.rearrange("(e p) d -> p e d", p=P)).then_inc(weights2_in, 16)

            load_block(0, 0, first=True)
            with strided(sp, 1, NB - 1, 2) as nb:
                for j in range(2):
                    load_block(nb + j, (1 + j) % 2)
            load_block(NB - 1, (NB - 1) % 2)
            sp.wait_ge(end_sb, 1)
            for i in range(4):
                sp.dma_start(x_buf[i], x_tiles[i]).then_inc(x_in[i], 16)

            def store(t, s):
                sp.wait_ge(fin_sb, t + 1)
                sp.dma_start(one(out_tiles, t), fin_buf[s % 2]).then_inc(stored[s % 2], 16)

            with strided(sp, 0, T - 4, 4) as t:
                for j in range(4):
                    store(t + j, j)
                    sp.dma_start(x_buf[j], one(x_tiles, t + (j + 4))).then_inc(x_in[j], 16)
            for t in range(T - 4, T):
                store(t, t)
            for i in range(2):
                sp.wait_ge(stored[i], 16 * (T // 2) + 16)

        @block.gpsimd
        def _(pool):
            nc.gpsimd.memset(v_acc, 0.0).then_inc(v_added, 2)
            def add_values(start, stop):
                with strided(pool, start, stop, 2) as b:
                    for j in range(2):
                        pool.wait_ge(v_in[j], b * 8 + 16)
                        pool.wait_ge(v_added, b + (j + 2))
                        nc.gpsimd.tensor_tensor(v_acc, v_acc, v_buf[j], ALU.add).then_inc(v_added, 1)

            add_values(0, 6)
            pool.wait_ge(prep_ps, 2 * DC + 5)
            pool.wait_ge(prep_sb, 2 * DC + 5)
            nc.gpsimd.memset(kv_flat, 0.0).then_inc(kv_zeroed, 1)
            add_values(6, 2 * NB)
            pool.wait_ge(kv_zeroed, 1)

            def gather(r, t, b, wait):
                n = r * T + t
                if wait:
                    wait_apart(pool, prodT_sb, n - (KV - 1))
                nc.gpsimd.tensor_copy(index_now[:, b, :], index[:, bass.ds(t, 1), :].rearrange("p a c -> p (a c)")
                                      ).then_inc(index_copied, 1)
                wait_apart(pool, index_copied, n + 1)
                for c in range(CH):
                    pool.indirect_dma_start(
                        adj_g[:, b, c, :], None, adj_cols,
                        bass.IndirectOffsetOnAxis(index_now[:, b, CH + c:CH + c + 1], 0),
                    ).then_inc(gathered[b], 16)
                if wait:
                    wait_apart(pool, pv_ps, n - (KV - 1))
                for c in range(CH):
                    pool.indirect_dma_start(
                        kv[:, b, c, :], None, kv_rows,
                        bass.IndirectOffsetOnAxis(index_now[:, b, c:c + 1], 0),
                        bounds_check=N - 1, oob_is_err=False,
                    ).then_inc(gathered[b], 16)

            def gather_round(r):
                wait_apart(pool, index_ready, r * (4 * CH) + 2 * CH)
                for t in range(KV + 2):
                    gather(r, t, t % KV, t >= KV)
                with strided(pool, KV + 2, HT - 2, KV) as t:
                    for j in range(KV):
                        gather(r, t + j, (KV + 2 + j) % KV, True)
                for t in range(HT - 2, HT + 1):
                    if t == HT:
                        wait_apart(pool, index_ready, r * (4 * CH) + 4 * CH)
                    gather(r, t, t % KV, True)
                with strided(pool, HT + 1, T, KV) as t:
                    for j in range(KV):
                        gather(r, t + j, (HT + 1 + j) % KV, True)

            gather_round(0)
            with more_rounds(pool) as r:
                gather_round(r)
            pool.wait_ge(end_sb, 1)
            with strided(pool, 0, T, 4) as t:
                for j in range(4):
                    pool.wait_ge(x_in[j], t * 4 + 16)
                    nc.gpsimd.tensor_tensor(x_buf[j], x_buf[j], beta[:, :], ALU.add).then_inc(xb_sb, 1)

        @block.tensor
        def _(pe):
            pe.sem_inc(joined_used, 2)
            pe.sem_inc(c_ps, 2)
            pe.wait_ge(cst_in, 16)
            pe.wait_ge(filled, FILLS)
            pe.wait_ge(weights_in, 32)

            def scan(nb, h, i):
                wait_apart(pe, joined_sb, nb * 8 + (i + 5))
                for gg in range(G8 // 2):
                    m = i * (G8 // 2) + gg
                    at = (127 - m + h * (NB // 2) * DC * G8) - nb * (DC * G8)
                    mm = nc.tensor.matmul(bank[h][:, :], cols(one_hot, at, P),
                                          joined[i % 2][:, gg * GK:(gg + 1) * GK],
                                          start=False, stop=False, skip_group_check=True)
                mm.then_inc(joined_used, 1)

            for h in range(2):
                nc.tensor.matmul(bank[h][:, 0:P], one_hot[:, P:2 * P], one_hot[:, P:2 * P], start=True, stop=False,
                                 skip_group_check=True)
            for a in range(DC):
                for e in range(DC):
                    mm = nc.tensor.matmul(bank[4 + a][:, :], w_left[:, e, a * P:(a + 1) * P], w_right[:, e, :],
                                          start=(e == 0), stop=(e == DC - 1))
                mm.then_inc(prep_ps, 1)
                scan(0, 0, a)
            bias = [cst[:, C_B + i * DC:C_B + (i + 1) * DC] for i in range(3)]
            for a in range(DC):
                for n, (w, b) in enumerate(((w_right, 0), (w_left, 1))):
                    for e in range(DC):
                        mm = nc.tensor.matmul(bank[2][:, n * DC + a:n * DC + a + 1], w[:, e, a * P:(a + 1) * P],
                                              bias[b][:, e:e + 1], start=(e == 0), stop=(e == DC - 1))
                    if a == DC - 1:
                        mm.then_inc(prep_ps, 1)
                scan(0, 0, DC + a)
            nc.tensor.matmul(bank[3][:, 0:DC], ones[:, :], small[:, 0:DC], start=True, stop=True
                             ).then_inc(prep_ps, 1)
            def project(nb, j, a):
                if a == 0:
                    pe.wait_ge(xT_in[j], nb * 8 + (16 - 8 * j))
                pe.wait_ge(q_sb, nb * DC + (a + 1))
                for d in range(DC):
                    mm = nc.tensor.matmul(bank[2 + a % 2][:, :], M[:, d, a * P:(a + 1) * P],
                                          xT_buf[j][:, d, :], start=(d == 0), stop=(d == DC - 1))
                mm.then_inc(q_ps, 1)

            def project_c(nb, j):
                pe.wait_ge(c_part_sb, nb * DC + DC)
                pe.wait_ge(c_sb, nb + 1)
                for k in range(4):
                    mm = nc.tensor.matmul(bank[4 + j][:, k:k + 1], c_part[:, k * P:(k + 1) * P], ones[:, 0:1],
                                          start=True, stop=True)
                mm.then_inc(c_ps, 1)

            for a in range(DC):
                scan(1, 0, 2 * a)
                scan(1, 0, 2 * a + 1)
                if a == 0:
                    pe.wait_ge(weights2_in, 32)
                    pe.wait_ge(prep_sb, DC + 3)
                for e in range(DC):
                    mm = nc.tensor.matmul(bank[4 + a][:, :], v_left[:, e, a * P:(a + 1) * P], m_right[:, e, :],
                                          start=(e == 0), stop=(e == DC - 1))
                mm.then_inc(prep_ps, 1)
                project(0, 0, a)
            pe.wait_ge(prep_sb, 2 * DC + 3)
            for e in range(DC):
                mm = nc.tensor.matmul(bank[6][0:1, :], bias[2][:, e:e + 1], m_right[:, e, :],
                                      start=(e == 0), stop=(e == DC - 1))
            mm.then_inc(prep_ps, 1)
            project_c(0, 0)
            pe.wait_ge(prep_sb, 2 * DC + 4)
            nc.tensor.matmul(bank[7][:, :], ones[0:1, :], beta_row, start=True, stop=True).then_inc(prep_ps, 1)

            def block_step(nb, j, h):
                for a in range(DC):
                    project(nb - 1, 1 - j, a)
                    scan(nb, h, 2 * a)
                    scan(nb, h, 2 * a + 1)
                project_c(nb - 1, 1 - j)

            for nb in range(2, NB // 2):
                block_step(nb, nb % 2, 0)
            with strided(pe, NB // 2, NB, 2) as nb:
                for j in range(2):
                    block_step(nb + j, j, 1)

            def spread_slots(r, h):
                for c in range(CH):
                    pe.wait_ge(spread_sb, r * (2 * CH) + (h * CH + c + 1))
                    nc.tensor.matmul(bank[6 + h][:, c * HT:(c + 1) * HT],
                                     spread[:, c, :, :].rearrange("p g s -> p (g s)"), tile_select,
                                     start=True, stop=True).then_inc(spread_ps, 1)

            pe.wait_ge(prep_sb, 2 * DC + 5)
            spread_slots(0, 0)
            for a in range(DC):
                project(NB - 1, 1, a)
            project_c(NB - 1, 1)
            pe.wait_ge(v_added, 2 + 2 * NB)
            pe.wait_ge(lead_sb, 5)
            for k in range(2):
                mm = nc.tensor.matmul(bank[0][:, :], ones[:, :], v_acc[:, k * D:(k + 1) * D],
                                      start=(k == 0), stop=(k == 1))
            mm.then_inc(lead_ps, 1)
            nc.tensor.matmul(bank[1][0:1, 0:P], small[:, 42:43], ident, start=True, stop=True).then_inc(lead_ps, 1)
            pe.wait_ge(q_sb, NB * DC + 2)
            pe.wait_ge(c_sb, NB + 2)
            pe.wait_ge(cuts_sb, 6)
            nc.tensor.transpose(bank[2][0:3 * T, 0:P], c_cuts[:, :, :].rearrange("p c t -> p (c t)"), ident
                                ).then_inc(lead_ps, 1)
            spread_slots(0, 1)

            def attend(r):
                wait_apart(pe, index_ready, r * (4 * CH) + 4 * CH)

                def step(t, third, s, new, mid, old):
                    n, p = r * T + t, s % 2

                    def keys(c):
                        if not (s < 1 and c < 2):
                            pe.wait_ge(keyT_sb, n * CH + (c - 1))
                        ps = bank[4 + (s * CH + c) % 2]
                        for a in range(DC):
                            mm = nc.tensor.transpose(ps[:, a * P:(a + 1) * P], kv[:, s % KV, c, a * P:(a + 1) * P],
                                                     ident)
                        mm.then_inc(keyT_ps, 1)

                    def scores(c):
                        pe.wait_ge(keyT_sb, n * CH + (c + 1))
                        ps = bank[6 + p][:, c * P:(c + 1) * P]
                        for a in range(DC):
                            mm = nc.tensor.matmul(ps, keyT[:, c, a * P:(a + 1) * P], cols(qT[:, a, :], t * P, P),
                                                  start=False, stop=(a == DC - 1), skip_group_check=True)
                        return mm

                    def values(c):
                        return nc.tensor.matmul(bank[2 + p][:, :], probT[:, p, c * P:(c + 1) * P],
                                                kv[:, (s - 2) % KV, c, D:2 * D], start=(c == 0), stop=(c == CH - 1))

                    if old:
                        pe.wait_ge(probT_sb, n - 1)
                        if s >= 4:
                            pe.wait_ge(o_sb, n - 3)
                        for c in range(CH - 1):
                            values(c)
                    if mid:
                        pe.wait_ge(prodT_sb, n)
                        if s >= 2:
                            pe.wait_ge(masked, n - 1)
                        for c in range(CH):
                            mm = nc.tensor.transpose(bank[0][:, c * P:(c + 1) * P],
                                                     prodT[:, 1 - p, c * P:(c + 1) * P], ident)
                        mm.then_inc(prod_ps, 1)
                    if old:
                        values(CH - 1).then_inc(pv_ps, 1)
                    if new:
                        pe.wait_ge(gathered[s % KV], (r * IN_BUF[s % KV] + (third + 1)) * (32 * CH))
                        keys(0)
                        keys(1)
                    if new:
                        pe.wait_ge(c_ready, n + 1)
                        if s >= 2:
                            pe.wait_ge(prodT_sb, n - 1)
                        nc.tensor.matmul(bank[6 + p][:, 0:SLOTS], ones_bf[:, :],
                                         c_tile[0:3 * T, p, :].unsqueeze(1).broadcast_to([3 * T, CH, P]),
                                         start=True, stop=False, skip_group_check=True)
                        scores(0)
                        keys(2)
                        scores(1)
                    if mid:
                        pe.wait_ge(weight_sb, n)
                        if s >= 2:
                            pe.wait_ge(probT_sb, n - 1)
                        for c in range(CH):
                            mm = nc.tensor.transpose(bank[1][:, c * P:(c + 1) * P], score[:, c * P:(c + 1) * P], ident)
                        mm.then_inc(probT_ps, 1)
                    if new:
                        scores(2).then_inc(score_ps, 1)

                tile_steps(pe, step)

            attend(0)
            with more_rounds(pe) as r:
                spread_slots(r, 0)
                spread_slots(r, 1)
                attend(r)

            def out_step(t, s, new, old):
                if new:
                    pe.wait_ge(on_sb, t + 1)
                    if s >= 2:
                        pe.wait_ge(onT_sb, t - 1)
                    for a in range(DC):
                        mm = nc.tensor.transpose(bank[4 + s % 2][:, a * P:(a + 1) * P],
                                                 on_buf[s % 2][:, a * P:(a + 1) * P], ident)
                    mm.then_inc(onT_ps, 1)
                if old:
                    pe.wait_ge(onT_sb, t)
                    if s >= 3:
                        pe.wait_ge(y_sb, t - 2)
                    for a in range(DC):
                        mm = nc.tensor.matmul(bank[6 + s % 2][:, :], onT_buf[(s - 1) % 2][:, a, :], G[:, a, :],
                                              start=(a == 0), stop=(a == DC - 1))
                    mm.then_inc(y_ps, 1)

            for t in range(4):
                out_step(t, t, True, t >= 1)
            with strided(pe, 4, T, 4) as t:
                for j in range(4):
                    out_step(t + j, 4 + j, True, True)
            out_step(T, 4, False, True)

        @block.scalar
        def _(act):
            act.sem_inc(q_sb, 2)
            act.sem_inc(c_sb, 2)
            act.wait_ge(prep_sb, DC + 3)
            with strided(act, 0, NB, 2) as nb:
                for j in range(2):
                    for a in range(DC):
                        act.wait_ge(q_ps, nb * DC + (DC * j + a + 1))
                        nc.scalar.activation(cols(qT[:, a, :], nb * 512 + 512 * j, 512), bank[2 + a % 2][:, :],
                                             ACT.Identity, bias=u_col[:, a:a + 1]).then_inc(q_sb, 1)
                    act.wait_ge(c_ps, nb + (j + 3))
                    nc.scalar.activation(cols(c_cols, nb * 4 + 4 * j, 4), bank[4 + j][:, 0:4],
                                         ACT.Identity, bias=kappa).then_inc(c_sb, 1)

            def attend(r, first):
                def size_of_scores(n):
                    act.wait_ge(prod_ps, n)
                    nc.scalar.activation(score, bank[0][:, 0:SLOTS], ACT.Abs).then_inc(abs_sb, 1)

                def step(t, third, s, new, mid, old):
                    n, p = r * T + t, s % 2

                    def copy_keys(c):
                        act.wait_ge(keyT_ps, n * CH + (c + 1))
                        if s >= 1:
                            act.wait_ge(score_ps, n)
                        nc.scalar.activation(keyT[:, c, :], bank[4 + (s * CH + c) % 2][:, :], ACT.Copy
                                             ).then_inc(keyT_sb, 1)

                    if mid:
                        size_of_scores(n)
                    if new:
                        copy_keys(0)
                        copy_keys(1)
                    if mid:
                        q = 1 - p
                        act.wait_ge(new_max_sb, n)
                        if not first:
                            nc.scalar.activation(alpha[:, q:q + 1], cols(neg_max, t - 1, 1), ACT.Exp,
                                                 bias=new_max[:, q:q + 1], scale=-1.0).then_inc(alpha_sb, 1)
                        nc.scalar.activation(p_rest[:, q:q + 1], cst[:, C_NEG:C_NEG + 1], ACT.Exp,
                                             bias=new_max[:, q:q + 1]).then_inc(exp_sb, 1)
                        nc.scalar.activation(score, score, ACT.Exp, bias=new_max[:, q:q + 1],
                                             accum_out=p_sum[:, q:q + 1]).then_inc(exp_sb, 1)
                    if new:
                        copy_keys(2)
                    if mid:
                        act.wait_ge(probT_ps, n)
                        if s >= 3:
                            act.wait_ge(pv_ps, n - 2)
                        nc.scalar.activation(probT[:, q, :], bank[1][:, 0:SLOTS], ACT.Copy).then_inc(probT_sb, 1)

                tile_steps(act, step)

            attend(0, True)
            with more_rounds(act) as r:
                attend(r, False)
            act.wait_ge(rest_sb, 1)
            nc.scalar.activation(p_all, neg_max[:, :], ACT.Exp, bias=cst[:, C_NEG:C_NEG + 1]).then_inc(end_exp, 1)

            def out_step(t, s, new, old):
                if new:
                    act.wait_ge(onT_ps, t + 1)
                    if s >= 2:
                        act.wait_ge(y_ps, t - 1)
                    nc.scalar.activation(onT_buf[s % 2].rearrange("p a r -> p (a r)"), bank[4 + s % 2][:, :], ACT.Copy
                                         ).then_inc(onT_sb, 1)
                if old:
                    act.wait_ge(mean_sb, t - 1)
                    nc.scalar.activation(std[:, s % 2:s % 2 + 1], mean_var[:, s % 2, 1:2], ACT.Sqrt,
                                         bias=cst[:, C_EPS:C_EPS + 1]).then_inc(std_sb, 1)

            for t in range(4):
                out_step(t, t, True, t >= 2)
            with strided(act, 4, T, 4) as t:
                for j in range(4):
                    out_step(t + j, 4 + j, True, True)
            out_step(T, 4, False, True)
            out_step(T + 1, 5, False, True)

        @block.vector
        def _(dve):
            dve.sem_inc(joined_sb, 4)
            dve.sem_inc(stored[0], 16)
            dve.sem_inc(stored[1], 16)
            nc.vector.memset(ones[:, :], 1.0).then_inc(filled, 1)
            nc.vector.memset(ones_bf[:, :], 1.0).then_inc(filled, 1)
            nc.vector.memset(one_hot, 0.0).then_inc(filled, 1)
            dve.wait_ge(filled, 3)
            nc.vector.memset(one_hot[:, 127:128], 1.0).then_inc(filled, 1)
            dve.wait_ge(cst_in, 16)
            nc.vector.tensor_tensor(small[:, 0:DC], cst[:, C_B:C_B + DC], cst[:, C_B + DC:C_B + 2 * DC], ALU.mult
                                    ).then_inc(filled, 1)

            def join(k, i):
                dve.wait_ge(adj_in[i], (k - i) * 4 + 16)
                dve.wait_ge(joined_used, k + 1)
                nc.vector.tensor_scalar(joined[i % 2], adj_buf[i], 0.0, None, ALU.not_equal
                                        ).then_inc(joined_sb, 1)

            def project_c(nb, j):
                dve.wait_ge(xT_in[j], nb * 8 + (16 - 8 * j))
                dve.wait_ge(prep_sb, DC + 3)
                dve.wait_ge(c_ps, nb + 2)
                for d in range(DC):
                    if d == 0:
                        nc.vector.tensor_scalar(c_part, xT_buf[j][:, d, :], w_col[:, d:d + 1], None, ALU.mult
                                                ).then_inc(c_part_sb, 1)
                    else:
                        dve.wait_ge(c_part_sb, nb * DC + d)
                        nc.vector.scalar_tensor_tensor(c_part, xT_buf[j][:, d, :], w_col[:, d:d + 1], c_part,
                                                       ALU.mult, ALU.add).then_inc(c_part_sb, 1)

            def join_block(nb, j):
                for i in range(8):
                    join(nb * 8 + i, i % 4)
                    if i == 4:
                        project_c(nb - 1, 1 - j)

            join(0, 0)
            for a in range(DC):
                join(a + 1, (a + 1) % 4)
                dve.wait_ge(prep_ps, a + 1)
                nc.vector.tensor_scalar(M[:, a, :], bank[4 + a][:, :], INV_SCALE, None, ALU.mult).then_inc(prep_sb, 1)
            for k in range(DC + 1, 2 * DC + 1):
                join(k, k % 4)
            dve.wait_ge(prep_ps, DC + 2)
            nc.vector.tensor_scalar(u_col, bank[2][:, 0:DC], INV_SCALE, None, ALU.mult).then_inc(prep_sb, 1)
            nc.vector.tensor_scalar(w_col, bank[2][:, DC:2 * DC], INV_SCALE, None, ALU.mult).then_inc(prep_sb, 1)
            dve.wait_ge(prep_ps, DC + 3)
            nc.vector.tensor_scalar(small[:, 8:8 + DC], bank[3][:, 0:DC], INV_SCALE, 0.0, ALU.mult, ALU.add,
                                    accum_out=kappa).then_inc(prep_sb, 1)
            join(9, 1)
            for a in range(DC):
                if a < DC - 1:
                    for k in (2 * a + 2, 2 * a + 3):
                        join(8 + k, k % 4)
                if a == 2:
                    project_c(0, 0)
                dve.wait_ge(prep_ps, DC + 4 + a)
                nc.vector.tensor_copy(G[:, a, :], bank[4 + a][:, :]).then_inc(prep_sb, 1)
            dve.wait_ge(prep_ps, 2 * DC + 4)
            dve.wait_ge(bm_in, 16)
            nc.vector.tensor_tensor(beta_row, bank[6][0:1, :], bm_row, ALU.add).then_inc(prep_sb, 1)
            dve.wait_ge(prep_ps, 2 * DC + 5)
            nc.vector.tensor_copy(beta[:, :], bank[7][:, :]).then_inc(prep_sb, 1)
            def number_joined(h):
                dve.wait_ge(joined_used, (h + 1) * (HALVES // 2) + 2)
                nc.vector.scalar_tensor_tensor(left[:, h, :], bank[h][:, :], 0.0, descending, ALU.is_gt, ALU.mult
                                               ).then_inc(lead_sb, 1)
                dve.wait_ge(lead_sb, 2 * h + 1)
                nc.vector.tensor_scalar(bank[h][:, :], left[:, h, :], 0.0, 0.0, ALU.is_gt, ALU.add,
                                        accum_out=small[:, 40 + h:41 + h]).then_inc(lead_sb, 1)
                dve.wait_ge(lead_sb, 2 * h + 2)

            def take(r, h):
                for i in range(0, GS, 8):
                    k = h * (TAKES // 2) + i // 4
                    if k:
                        wait_apart(dve, took, r * TAKES + k)
                    nc.vector.max(slots[:, h, i:i + 8], left[:, h, :]).then_inc(took, 1)
                    wait_apart(dve, took, r * TAKES + (k + 1))
                    nc.vector.match_replace(left[:, h, :], slots[:, h, i:i + 8], left[:, h, :], 0.0
                                            ).then_inc(took, 1)
                for c in range(CH):
                    nc.vector.tensor_tensor(spread[:, c, :, :], group_mask,
                                            slots[:, h, c * SPC:(c + 1) * SPC].unsqueeze(1)
                                            .broadcast_to([P, G8, SPC]), ALU.mult).then_inc(spread_sb, 1)

            def index_slots(r, h):
                dve.wait_ge(spread_ps, r * (2 * CH) + (h + 1) * CH)
                tiles = slice(h * HT, (h + 1) * HT)
                for c in range(CH):
                    v = bank[6 + h][:, c * HT:(c + 1) * HT]
                    nc.vector.tensor_scalar(index[:, tiles, c], v, -float(G8), cst[:, C_BK:C_BK + 1],
                                            ALU.mult, ALU.add).then_inc(index_ready, 1)
                    nc.vector.scalar_tensor_tensor(index[:, tiles, CH + c], v, -float(G8 * T),
                                                   cst[:, C_BA + h * HT:C_BA + (h + 1) * HT],
                                                   ALU.mult, ALU.add).then_inc(index_ready, 1)

            for nb in range(2, NB // 2):
                join_block(nb, nb % 2)
            number_joined(0)
            take(0, 0)
            with strided(dve, NB // 2, NB, 2) as nb:
                for j in range(2):
                    join_block(nb + j, j)
            index_slots(0, 0)
            project_c(NB - 1, 1)
            number_joined(1)
            nc.vector.tensor_tensor(small[:, 42:43], small[:, 40:41], small[:, 41:42], ALU.max).then_inc(lead_sb, 1)
            take(0, 1)
            dve.wait_ge(c_sb, NB + 2)
            for k in range(2):
                rest = c_cuts[:, 2, :] if k else c_cols[:, :]
                if k:
                    dve.wait_ge(cuts_sb, 3)
                nc.vector.tensor_copy(c_cut[:, :], rest).then_inc(cuts_sb, 1)
                dve.wait_ge(cuts_sb, 3 * k + 1)
                nc.vector.tensor_copy(c_cuts[:, k, :], c_cut[:, :]).then_inc(cuts_sb, 1)
                dve.wait_ge(cuts_sb, 3 * k + 2)
                nc.vector.tensor_tensor(c_cuts[:, 2, :], rest, c_cuts[:, k, :], ALU.subtract).then_inc(cuts_sb, 1)
            dve.wait_ge(lead_ps, 1)
            nc.vector.tensor_copy(vsum[:, :], bank[0][:, :]).then_inc(lead_sb, 1)
            dve.wait_ge(lead_ps, 2)
            nc.vector.tensor_reduce(small[0:1, 43:44], bank[1][0:1, 0:P], AX_X, ALU.max).then_inc(lead_sb, 1)
            dve.wait_ge(lead_ps, 3)
            nc.vector.tensor_copy(c_rows[:, :], bank[2][0:3 * T, 0:P]).then_inc(lead_sb, 1)
            index_slots(0, 1)
            dve.wait_ge(lead_sb, 8)
            nc.vector.tensor_scalar(small[0:1, 44:44 + MAXR - 1], cst[0:1, C_THR:C_THR + MAXR - 1], small[0:1, 43:44],
                                    0.0, ALU.is_lt, ALU.add, accum_out=small[0:1, 60:61]).then_inc(lead_sb, 1)
            dve.wait_ge(lead_sb, 9)
            nc.vector.tensor_copy(rounds_i[:, :], small[0:1, 60:61]).then_inc(rounds_ready, 1)

            def attend(r, first):
                def step(t, third, s, new, mid, old):
                    n, p = r * T + t, s % 2
                    if new:
                        nc.vector.tensor_scalar(c_tile[0:3 * T, p, :], c_rows[:, :], cols(cut_select, t, 1), None,
                                                ALU.mult).then_inc(c_ready, 1)
                    if mid:
                        q = 1 - p
                        dve.wait_ge(prod_ps, n)
                        prod = bank[0][:, 0:SLOTS]
                        dve.wait_ge(abs_sb, n)
                        nc.vector.tensor_scalar(score, score, TINY, MASKED, ALU.is_lt, ALU.mult
                                                ).then_inc(tiny_sb, 1)
                        dve.wait_ge(tiny_sb, n)
                        nc.vector.tensor_tensor(score, score, prod, ALU.add).then_inc(masked, 1)
                        dve.wait_ge(masked, n)
                        nc.vector.tensor_reduce(chunk_max[:, q:q + 1], score, AX_X, ALU.max, negate=True
                                                ).then_inc(max_sb, 1)
                        dve.wait_ge(max_sb, n)
                        if first:
                            nc.vector.tensor_scalar(new_max[:, q:q + 1], chunk_max[:, q:q + 1], -MASKED, None,
                                                    ALU.min).then_inc(new_max_sb, 1)
                        else:
                            nc.vector.tensor_tensor(new_max[:, q:q + 1], chunk_max[:, q:q + 1],
                                                    cols(neg_max, t - 1, 1), ALU.min).then_inc(new_max_sb, 1)
                    if old:
                        dve.wait_ge(pv_ps, n - 1)
                        acc = O[:, bass.ds(t - 2, 1), :].rearrange("p a d -> p (a d)")
                        if first:
                            nc.vector.tensor_copy(acc, bank[2 + p][:, :]).then_inc(o_sb, 1)
                        else:
                            nc.vector.scalar_tensor_tensor(acc, acc, alpha[:, p:p + 1], bank[2 + p][:, :],
                                                           ALU.mult, ALU.add).then_inc(o_sb, 1)
                    if mid:
                        dve.wait_ge(exp_sb, n * 2)
                        nc.vector.tensor_scalar(score, score, p_rest[:, q:q + 1], None, ALU.subtract
                                                ).then_inc(weight_sb, 1)
                        l = cols(denom, t - 1, 1)
                        nc.vector.scalar_tensor_tensor(l if first else l_add[:, q:q + 1], p_rest[:, q:q + 1],
                                                       -float(SLOTS), p_sum[:, q:q + 1], ALU.mult, ALU.add
                                                       ).then_inc(denom_sb if first else sum_sb, 1)
                        if not first:
                            dve.wait_ge(alpha_sb, n - T)
                            dve.wait_ge(sum_sb, n - T)
                            nc.vector.scalar_tensor_tensor(l, l, alpha[:, q:q + 1], l_add[:, q:q + 1],
                                                           ALU.mult, ALU.add).then_inc(denom_sb, 1)
                        nc.vector.tensor_copy(cols(neg_max, t - 1, 1), new_max[:, q:q + 1]).then_inc(state_sb, 1)
                    if new:
                        dve.wait_ge(score_ps, n + 1)
                        nc.vector.tensor_tensor(prodT[:, p, :], bank[6 + p][:, 0:SLOTS],
                                                adj_g[:, s % KV, :, :].rearrange("p c r -> p (c r)"), ALU.mult
                                                ).then_inc(prodT_sb, 1)

                tile_steps(dve, step)
                dve.wait_ge(o_sb, r * T + T)
                dve.wait_ge(denom_sb, r * T + T)
                dve.wait_ge(state_sb, r * T + T)

            attend(0, True)
            with more_rounds(dve) as r:
                for h in range(2):
                    take(r, h)
                    index_slots(r, h)
                attend(r, False)
            dve.sem_inc(rest_sb, 1)
            dve.sem_inc(end_sb, 1)
            dve.wait_ge(end_exp, 1)
            nc.vector.scalar_tensor_tensor(denom[:, :], p_all, float(N), denom[:, :], ALU.mult, ALU.add
                                           ).then_inc(end_l, 1)
            dve.wait_ge(end_l, 1)
            nc.vector.reciprocal(r_denom[:, :], denom[:, :]).then_inc(end_l, 1)
            dve.wait_ge(end_l, 2)

            def out_step(t, s, new, mid, old):
                if new:
                    if s >= 2:
                        dve.wait_ge(onT_ps, t - 1)
                    nc.vector.scalar_tensor_tensor(on_buf[s % 2], vsum[:, :], cols(p_all, t, 1),
                                                   O[:, bass.ds(t, 1), :].rearrange("p a d -> p (a d)"),
                                                   ALU.mult, ALU.add).then_inc(on_sb, 1)
                if mid:
                    b = s % 2
                    dve.wait_ge(y_ps, t - 1)
                    dve.wait_ge(xb_sb, t - 1)
                    if s >= 4:
                        dve.wait_ge(fin_sb, t - 3)
                    nc.vector.scalar_tensor_tensor(y_buf[b], bank[6 + (s + 1) % 2][:, :], cols(r_denom, t - 2, 1),
                                                   x_buf[(s - 2) % 4], ALU.mult, ALU.add).then_inc(y_sb, 1)
                    dve.wait_ge(y_sb, t - 1)
                    nc.vector.bn_stats(stats[:, b, :], y_buf[b]).then_inc(stats_sb, 1)
                    wait_apart(dve, stats_sb, t - 1)
                    nc.vector.bn_aggr(mean_var[:, b, :], stats[:, b, :]).then_inc(mean_sb, 1)
                if old:
                    b = (s - 3) % 2
                    dve.wait_ge(std_sb, t - 2)
                    nc.vector.reciprocal(rstd[:, b:b + 1], std[:, b:b + 1]).then_inc(rstd_sb, 1)
                    dve.wait_ge(rstd_sb, t - 2)
                    dve.wait_ge(stored[b], (t - s) * 8 + (16 * ((s - 3) // 2) + 16))
                    nc.vector.tensor_scalar(fin_buf[b], y_buf[b], mean_var[:, b, 0:1], rstd[:, b:b + 1],
                                            ALU.subtract, ALU.mult).then_inc(fin_sb, 1)

            for t in range(4):
                out_step(t, t, True, t >= 2, t >= 3)
            with strided(dve, 4, T, 4) as t:
                for j in range(4):
                    out_step(t + j, 4 + j, True, True, True)
            for t in range(T, T + 3):
                out_step(t, t, False, t < T + 2, True)


def layout(adj, key, value, x, Wq, Wk, Wv, Wm, bq, bk, bv, bm):
    import numpy as np

    a = adj.reshape(P, T, GK, 2, G8 // 2)
    const = np.zeros((P, C_ALL), np.float32)
    p = np.arange(P)
    const[:, C_ID:C_ID + P] = np.eye(P)
    const[:, C_DESC:C_DESC + GK] = GK - np.arange(GK)
    const[:, C_GRP:C_GRP + P] = (p % G8)[:, None] == (p // SPC)[None, :]
    const[:, C_SEL:C_SEL + HT] = (p // G8)[:, None] == np.arange(HT)[None, :]
    const[:, C_BK] = N + p // SPC
    const[:, C_BA:C_BA + T] = (T * (N + p // SPC))[:, None] + np.arange(T)[None, :]
    const[:, C_THR:C_THR + MAXR - 1] = [GS * q for q in range(1, MAXR)]
    const[:, C_NEG] = MASKED
    const[:, C_EPS] = 1e-5
    const[:3 * T, C_CUT:C_CUT + T] = np.tile(np.eye(T), (3, 1))
    for i, b in enumerate((bq, bk, bv)):
        const[:, C_B + i * DC:C_B + (i + 1) * DC] = b.reshape(DC, P).T
    return {
        "adj_tiles": np.ascontiguousarray(a.transpose(1, 3, 0, 4, 2)).reshape(HALVES, P, N // 2),
        "adj_cols": np.concatenate([adj.reshape(P, T, N).transpose(2, 1, 0).reshape(N * T, P),
                                    np.zeros((G8 * T, P), adj.dtype)]),
        "kv_rows": np.concatenate([key, value], axis=1),
        "value": value,
        "x": x,
        "xT": np.ascontiguousarray(x.reshape(P, NB, T // NB, DC, P).transpose(1, 4, 3, 2, 0)).reshape(NB, P, DC, 512),
        "wq": Wq, "wk": Wk, "wv": Wv, "wmT": np.ascontiguousarray(Wm.T),
        "bm": bm.reshape(1, D),
        "consts": const,
    }


def kernel(x, adj, L0_gnn_key, L0_gnn_value, L0_gnn_Wq, L0_gnn_bq, L0_gnn_Wk, L0_gnn_bk, L0_gnn_Wv, L0_gnn_bv,
           L0_gnn_Wm, L0_gnn_bm):
    import numpy as np
    import concourse.bacc as bacc
    from concourse.bass_utils import run_bass_kernel_spmd

    given = [np.asarray(i) for i in (adj, L0_gnn_key, L0_gnn_value, x, L0_gnn_Wq, L0_gnn_Wk, L0_gnn_Wv, L0_gnn_Wm,
                                     L0_gnn_bq, L0_gnn_bk, L0_gnn_bv, L0_gnn_bm)]
    arrays = layout(*given)
    nc = bacc.Bacc("TRN2", target_bir_lowering=False, num_devices=1)
    args = {n: nc.dram_tensor(n, a.shape, mybir.dt.from_np(a.dtype), kind="ExternalInput").ap()
            for n, a in arrays.items()}
    out = nc.dram_tensor("out", (N, D), F32, kind="ExternalOutput").ap()
    build(nc, out=out, **args)
    r = run_bass_kernel_spmd(nc, [arrays], core_ids=[0])
    return r.results[0]["out"]
```

```python
from contextlib import ExitStack, contextmanager

import concourse.bass as bass
from concourse import mybir

F32 = mybir.dt.float32
BF16 = mybir.dt.bfloat16
I32 = mybir.dt.int32
ALU = mybir.AluOpType
ACT = mybir.ActivationFunctionType
AX_X = mybir.AxisListType.X

P = 128
N = 4096
D = 512
DC = D // P
T = N // P
HT = T // 2
G8 = P // HT
GK = N // G8
CH = 3
SLOTS = CH * P
GS = SLOTS // G8
SPC = P // G8
MAXR = -(-GK // GS)
NB = N // 512
HALVES = 2 * T
KV = 3
INV_SCALE = 1.0 / float(N) ** 0.5
MASKED = -1e9
TINY = 1e-5

C_ID = 0
C_DESC = C_ID + P
C_GRP = C_DESC + GK
C_SEL = C_GRP + P
C_BK = C_SEL + HT
C_BA = C_BK + 1
C_THR = C_BA + T
C_NEG = C_THR + MAXR - 1
C_EPS = C_NEG + 1
C_B = C_EPS + 1
C_ALL = C_B + 3 * DC


@contextmanager
def strided(eng, start, stop, step):
    with eng.Fori(0, (stop - start) // step) as m:
        yield m * step + start


def build(nc, adj_tiles, adj_cols, kv_rows, value, x, xT, wq, wk, wv, wmT, bm, consts, out):
    with ExitStack() as ctx:
        def sb(name, shape, dt=F32):
            return ctx.enter_context(nc.sbuf_tensor(name, shape, dt))

        def sem(name):
            return ctx.enter_context(nc.semaphore(name))

        bank = [ctx.enter_context(nc.psum_tensor(f"bank{i}", [P, 512], F32)) for i in range(8)]

        cst = sb("cst", [P, C_ALL])
        ident = cst[:, C_ID:C_ID + P]
        descending = cst[:, C_DESC:C_DESC + GK]
        group_mask = cst[:, C_GRP:C_GRP + P].rearrange("p (g s) -> p g s", g=G8)
        tile_select = cst[:, C_SEL:C_SEL + HT]
        qT = sb("qT", [P, DC, N])
        G = sb("G", [P, DC, D])
        beta = sb("beta", [P, D])
        vsum = sb("vsum", [P, D])
        ones = sb("ones", [P, P])
        left = sb("left", [P, 2, GK])
        c_cols = sb("c_cols", [P, T])
        slots = sb("slots", [P, 2, GS])
        index = sb("index", [P, T, 2 * CH], I32)
        neg_max = sb("neg_max", [P, T])
        denom = sb("denom", [P, T])
        small = sb("small", [P, 64])
        rounds_i = sb("rounds_i", [1, 1], I32)

        O = sb("O", [P, T, D])
        o_flat = O[:, :, :].rearrange("p t d -> p (t d)")
        adj_buf = [o_flat[:, i * 2048:(i + 1) * 2048] for i in range(4)]
        joined = [o_flat[:, 8192 + i * 1024:8192 + (i + 1) * 1024].bitcast(BF16) for i in range(2)]
        xT_buf = [o_flat[:, 10240 + i * 2048:10240 + (i + 1) * 2048].rearrange("p (d n) -> p d n", d=DC)
                  for i in range(2)]
        v_acc = o_flat[:, 13312:13312 + 2 * D]
        v_buf = [o_flat[:, 14336 + i * 1024:14336 + (i + 1) * 1024] for i in range(2)]

        kv = sb("kv", [P, KV, CH, 2 * D])
        kv_flat = kv[:, :, :, :].rearrange("p b c d -> p (b c d)")
        w_left = kv_flat[:, 0:2048].rearrange("p (e d) -> p e d", e=DC)
        w_right = kv_flat[:, 2048:4096].rearrange("p (e d) -> p e d", e=DC)
        v_left = kv_flat[:, 5120:7168].rearrange("p (e d) -> p e d", e=DC)
        m_right = kv_flat[:, 7168:9216].rearrange("p (e d) -> p e d", e=DC)
        beta_row = kv_flat[0:1, 4096:4096 + D]
        bm_row = kv_flat[0:1, 4608:4608 + D]

        adj_g = sb("adj_g", [P, KV, CH, P])
        keyT = sb("keyT", [P, DC, SLOTS])
        keyT_flat = keyT[:, :, :].rearrange("p a s -> p (a s)")
        c_part = keyT_flat[:, 2 * D:3 * D]
        work = sb("work", [P, 2064])
        probT = work[:, 0:2 * SLOTS].rearrange("p (b s) -> p b s", b=2)
        score = work[:, 2 * SLOTS:3 * SLOTS]
        size = work[:, 3 * SLOTS:4 * SLOTS]
        q_tile = work[:, 4 * SLOTS:4 * SLOTS + D].rearrange("p (a r) -> p a r", a=DC)
        M = work[:, 0:DC * D].rearrange("p (a d) -> p a d", a=DC)
        u_col = work[:, 2048:2052]
        w_col = work[:, 2052:2056]
        kappa = work[:, 2056:2057]
        adjT = sb("adjT", [P, SLOTS])
        spread = adjT[:, :].rearrange("p (c g s) -> p c g s", c=CH, g=G8)
        one_hot = sb("one_hot", [P, 2 * P], BF16)[:, :]
        index_now = sb("index_now", [P, KV, 2 * CH], I32)
        chunk_max = sb("chunk_max", [P, 2])
        new_max = sb("new_max", [P, 2])
        alpha = sb("alpha", [P, 2])
        p_rest = sb("p_rest", [P, 2])
        p_sum = sb("p_sum", [P, 2])
        l_add = sb("l_add", [P, 2])

        x_buf = [kv_flat[:, i * 512:(i + 1) * 512] for i in range(4)]
        on_buf = [kv_flat[:, 3072 + i * 512:3072 + (i + 1) * 512] for i in range(2)]
        onT_buf = [kv_flat[:, 4096 + i * 512:4096 + (i + 1) * 512].rearrange("p (a r) -> p a r", a=DC)
                   for i in range(2)]
        y_buf = [kv_flat[:, 5120 + i * 512:5120 + (i + 1) * 512] for i in range(2)]
        fin_buf = [kv_flat[:, 6144 + i * 512:6144 + (i + 1) * 512] for i in range(2)]
        stats = kv_flat[:, 7168:7180].rearrange("p (b s) -> p b s", b=2)
        mean_var = kv_flat[:, 7184:7188].rearrange("p (b s) -> p b s", b=2)
        std = kv_flat[:, 7192:7194]
        rstd = kv_flat[:, 7200:7202]
        p_all = small[:, 0:T]
        r_denom = denom

        cst_in = sem("cst_in")
        passed = sem("passed")
        weights_in = sem("weights_in")
        weights2_in = sem("weights2_in")
        bm_in = sem("bm_in")
        filled = sem("filled")
        prep_ps = sem("prep_ps")
        prep_sb = sem("prep_sb")
        adj_in = [sem(f"adj_in{i}") for i in range(4)]
        xT_in = [sem(f"xT_in{i}") for i in range(2)]
        v_in = [sem(f"v_in{i}") for i in range(2)]
        v_added = sem("v_added")
        v_zeroed = sem("v_zeroed")
        vsum_ps = sem("vsum_ps")
        vsum_sb = sem("vsum_sb")
        joined_sb = sem("joined_sb")
        joined_used = sem("joined_used")
        q_ps = sem("q_ps")
        q_sb = sem("q_sb")
        c_part_sb = sem("c_part_sb")
        c_ps = sem("c_ps")
        c_sb = sem("c_sb")
        lead_sb = sem("lead_sb")
        lead_ps = sem("lead_ps")
        kv_zeroed = sem("kv_zeroed")
        rounds_ready = sem("rounds_ready")
        took = sem("took")
        spread_sb = sem("spread_sb")
        spread_ps = sem("spread_ps")
        index_ready = sem("index_ready")
        index_copied = sem("index_copied")
        adj_gathered = [sem(f"adj_gathered{i}") for i in range(KV)]
        gathered = [sem(f"gathered{i}") for i in range(KV)]
        adjT_ps = sem("adjT_ps")
        adjT_sb = sem("adjT_sb")
        q_tile_sb = sem("q_tile_sb")
        keyT_ps = sem("keyT_ps")
        keyT0_sb = sem("keyT0_sb")
        keyT_sb = sem("keyT_sb")
        score_ps = sem("score_ps")
        prod_sb = sem("prod_sb")
        abs_sb = sem("abs_sb")
        tiny_sb = sem("tiny_sb")
        masked = sem("masked")
        max_sb = sem("max_sb")
        new_max_sb = sem("new_max_sb")
        alpha_sb = sem("alpha_sb")
        exp_sb = sem("exp_sb")
        weight_sb = sem("weight_sb")
        sum_sb = sem("sum_sb")
        denom_sb = sem("denom_sb")
        state_sb = sem("state_sb")
        probT_ps = sem("probT_ps")
        probT_sb = sem("probT_sb")
        pv_ps = sem("pv_ps")
        o_sb = sem("o_sb")
        rest_sb = sem("rest_sb")
        end_sb = sem("end_sb")
        end_exp = sem("end_exp")
        end_l = sem("end_l")
        x_in = [sem(f"x_in{i}") for i in range(4)]
        xb_sb = sem("xb_sb")
        on_sb = sem("on_sb")
        onT_ps = sem("onT_ps")
        onT_sb = sem("onT_sb")
        y_ps = sem("y_ps")
        y_sb = sem("y_sb")
        stats_sb = sem("stats_sb")
        mean_sb = sem("mean_sb")
        std_sb = sem("std_sb")
        rstd_sb = sem("rstd_sb")
        fin_sb = sem("fin_sb")
        stored = [sem(f"stored{i}") for i in range(2)]

        FILLS = 4
        TAKES = 4 * GS // 8
        x_tiles = x.rearrange("(r t) d -> t r d", t=T)
        out_tiles = out.rearrange("(r t) d -> t r d", t=T)
        v_rows = value.rearrange("(b p k) d -> b p (k d)", p=P, k=2)

        key_bank = (bank[4], bank[5], bank[7])

        def one(ap, i):
            return ap[bass.ds(i, 1)].rearrange("a p n -> p (a n)")

        def cols(ap, start, n):
            return ap[:, bass.ds(start, n)]

        def wait_apart(eng, s, value):
            eng.wait_ge(s, value)
            eng.sem_inc(passed, 1)

        def tile_steps(eng, step):
            step(0, 0, 0, True, False, False)
            step(1, 0, 1, True, True, False)
            with eng.Fori(0, (T - 2) // 6) as m:
                for j in range(6):
                    step(m * 6 + (2 + j), m * 2 + (2 + j) // KV, 2 + j, True, True, True)
            step(T, T // KV, T % 6, False, True, True)
            step(T + 1, (T + 1) // KV, (T + 1) % 6, False, False, True)

        def first_tile_steps(eng, step, between):
            step(0, 0, 0, True, False, False)
            step(1, 0, 1, True, True, False)
            with eng.Fori(0, 2) as m:
                for j in range(6):
                    step(m * 6 + (2 + j), m * 2 + (2 + j) // KV, 2 + j, True, True, True)
            for t in range(14, 20):
                step(t, t // KV, t, True, True, True)
            between()
            with eng.Fori(0, (T - 20) // 6) as m:
                for j in range(6):
                    step(m * 6 + (20 + j), m * 2 + (20 + j) // KV, 20 + j, True, True, True)
            step(T, T // KV, T % 6, False, True, True)
            step(T + 1, (T + 1) // KV, (T + 1) % 6, False, False, True)

        @contextmanager
        def more_rounds(eng):
            eng.wait_ge(rounds_ready, 1)
            n = eng.value_load(rounds_i[0:1, 0:1], min_val=0, max_val=MAXR - 1)
            with eng.If(n > 0):
                with eng.Fori(0, n) as m:
                    yield m + 1

        IN_BUF = [len(range(b, T, KV)) for b in range(KV)]

        block = ctx.enter_context(nc.Block())

        @block.sync
        def _(sp):
            sp.dma_start(w_left, wq.rearrange("(e p) d -> p e d", p=P)).then_inc(weights_in, 16)
            sp.dma_start(w_right, wk.rearrange("(e p) d -> p e d", p=P)).then_inc(weights_in, 16)
            sp.dma_start(cst[:, :], consts).then_inc(cst_in, 16)
            sp.dma_start(bm_row, bm).then_inc(bm_in, 16)
            def load_xT(nb, j):
                sp.wait_ge(c_ps, nb + 1)
                sp.dma_start(xT_buf[j], xT[bass.ds(nb, 1)].rearrange("a p d n -> p (a d) n")
                             ).then_inc(xT_in[j], 16)

            def load_block(nb, j, first=False):
                for i in range(8):
                    sp.wait_ge(joined_sb, nb * 8 + (i + 1))
                    sp.dma_start(adj_buf[i % 4], one(adj_tiles, nb * 8 + i)).then_inc(adj_in[i % 4], 16)
                    if i == 3:
                        load_xT(nb, j)
                    if i == 5 and first:
                        sp.dma_start(v_left, wv.rearrange("(e p) d -> p e d", p=P)).then_inc(weights2_in, 16)
                        sp.dma_start(m_right, wmT.rearrange("(e p) d -> p e d", p=P)).then_inc(weights2_in, 16)

            load_block(0, 0, first=True)
            with strided(sp, 1, NB - 1, 2) as nb:
                for j in range(2):
                    load_block(nb + j, (1 + j) % 2)
            load_block(NB - 1, (NB - 1) % 2)
            with strided(sp, 0, 2 * NB, 2) as b:
                for i in range(2):
                    sp.wait_ge(v_added, b + (i + 1))
                    sp.dma_start(v_buf[i], one(v_rows, b + i)).then_inc(v_in[i], 16)
            sp.wait_ge(end_sb, 1)
            for i in range(4):
                sp.dma_start(x_buf[i], x_tiles[i]).then_inc(x_in[i], 16)

            def store(t, s):
                sp.wait_ge(fin_sb, t + 1)
                sp.dma_start(one(out_tiles, t), fin_buf[s % 2]).then_inc(stored[s % 2], 16)

            with strided(sp, 0, T - 4, 4) as t:
                for j in range(4):
                    store(t + j, j)
                    sp.dma_start(x_buf[j], one(x_tiles, t + (j + 4))).then_inc(x_in[j], 16)
            for t in range(T - 4, T):
                store(t, t)
            for i in range(2):
                sp.wait_ge(stored[i], 16 * (T // 2) + 16)

        @block.gpsimd
        def _(pool):
            pool.wait_ge(prep_ps, 2 * DC + 5)
            pool.wait_ge(prep_sb, 2 * DC + 5)
            nc.gpsimd.memset(kv_flat, 0.0).then_inc(kv_zeroed, 1)
            pool.wait_ge(kv_zeroed, 1)

            def gather(r, t, b, wait):
                n = r * T + t
                if wait:
                    wait_apart(pool, adjT_ps, n - (KV - 1))
                nc.gpsimd.tensor_copy(index_now[:, b, :], index[:, bass.ds(t, 1), :].rearrange("p a c -> p (a c)")
                                      ).then_inc(index_copied, 1)
                wait_apart(pool, index_copied, n + 1)
                for c in range(CH):
                    pool.indirect_dma_start(
                        adj_g[:, b, c, :], None, adj_cols,
                        bass.IndirectOffsetOnAxis(index_now[:, b, CH + c:CH + c + 1], 0),
                    ).then_inc(adj_gathered[b], 16)
                if wait:
                    wait_apart(pool, pv_ps, n - (KV - 1))
                for c in range(CH):
                    pool.indirect_dma_start(
                        kv[:, b, c, :], None, kv_rows,
                        bass.IndirectOffsetOnAxis(index_now[:, b, c:c + 1], 0),
                        bounds_check=N - 1, oob_is_err=False,
                    ).then_inc(gathered[b], 16)

            def gather_round(r):
                wait_apart(pool, index_ready, r * (4 * CH) + 2 * CH)
                for t in range(KV + 2):
                    gather(r, t, t % KV, t >= KV)
                with strided(pool, KV + 2, HT - 2, KV) as t:
                    for j in range(KV):
                        gather(r, t + j, (KV + 2 + j) % KV, True)
                for t in range(HT - 2, HT + 1):
                    if t == HT:
                        wait_apart(pool, index_ready, r * (4 * CH) + 4 * CH)
                    gather(r, t, t % KV, True)
                with strided(pool, HT + 1, T, KV) as t:
                    for j in range(KV):
                        gather(r, t + j, (HT + 1 + j) % KV, True)

            gather_round(0)
            with more_rounds(pool) as r:
                gather_round(r)
            pool.wait_ge(end_sb, 1)
            with strided(pool, 0, T, 4) as t:
                for j in range(4):
                    pool.wait_ge(x_in[j], t * 4 + 16)
                    nc.gpsimd.tensor_tensor(x_buf[j], x_buf[j], beta[:, :], ALU.add).then_inc(xb_sb, 1)

        @block.tensor
        def _(pe):
            pe.sem_inc(joined_used, 2)
            pe.sem_inc(c_ps, 2)
            pe.wait_ge(filled, FILLS - 1)
            pe.wait_ge(weights_in, 32)

            def scan(nb, h, i):
                wait_apart(pe, joined_sb, nb * 8 + (i + 5))
                for gg in range(G8 // 2):
                    m = i * (G8 // 2) + gg
                    at = (127 - m + h * (NB // 2) * DC * G8) - nb * (DC * G8)
                    mm = nc.tensor.matmul(bank[h][:, :], cols(one_hot, at, P),
                                          joined[i % 2][:, gg * GK:(gg + 1) * GK],
                                          start=False, stop=False, skip_group_check=True)
                mm.then_inc(joined_used, 1)

            for h in range(2):
                nc.tensor.matmul(bank[h][:, 0:P], one_hot[:, P:2 * P], one_hot[:, P:2 * P], start=True, stop=False,
                                 skip_group_check=True)
            for a in range(DC):
                for e in range(DC):
                    mm = nc.tensor.matmul(bank[4 + a][:, :], w_left[:, e, a * P:(a + 1) * P], w_right[:, e, :],
                                          start=(e == 0), stop=(e == DC - 1))
                mm.then_inc(prep_ps, 1)
                scan(0, 0, a)
            bias = [cst[:, C_B + i * DC:C_B + (i + 1) * DC] for i in range(3)]
            pe.wait_ge(cst_in, 16)
            pe.wait_ge(filled, FILLS)
            for a in range(DC):
                for n, (w, b) in enumerate(((w_right, 0), (w_left, 1))):
                    for e in range(DC):
                        mm = nc.tensor.matmul(bank[2][:, n * DC + a:n * DC + a + 1], w[:, e, a * P:(a + 1) * P],
                                              bias[b][:, e:e + 1], start=(e == 0), stop=(e == DC - 1))
                    if a == DC - 1:
                        mm.then_inc(prep_ps, 1)
                scan(0, 0, DC + a)
            nc.tensor.matmul(bank[3][:, 0:DC], ones[:, :], small[:, 0:DC], start=True, stop=True
                             ).then_inc(prep_ps, 1)
            def project(nb, j, a):
                if a == 0:
                    pe.wait_ge(xT_in[j], nb * 8 + (16 - 8 * j))
                pe.wait_ge(q_sb, nb * DC + (a + 1))
                for d in range(DC):
                    mm = nc.tensor.matmul(bank[2 + a % 2][:, :], M[:, d, a * P:(a + 1) * P],
                                          xT_buf[j][:, d, :], start=(d == 0), stop=(d == DC - 1))
                mm.then_inc(q_ps, 1)

            def project_c(nb, j):
                pe.wait_ge(c_part_sb, nb * DC + DC)
                pe.wait_ge(c_sb, nb + 1)
                for k in range(4):
                    mm = nc.tensor.matmul(bank[4 + j][:, k:k + 1], c_part[:, k * P:(k + 1) * P], ones[:, 0:1],
                                          start=True, stop=True)
                mm.then_inc(c_ps, 1)

            def product_G(a):
                for e in range(DC):
                    mm = nc.tensor.matmul(bank[4 + a][:, :], v_left[:, e, a * P:(a + 1) * P], m_right[:, e, :],
                                          start=(e == 0), stop=(e == DC - 1))
                mm.then_inc(prep_ps, 1)

            for a in range(DC):
                scan(1, 0, 2 * a)
                scan(1, 0, 2 * a + 1)
                if a == 0:
                    pe.wait_ge(weights2_in, 32)
                    pe.wait_ge(prep_sb, DC + 3)
                if a < 2:
                    product_G(a)
                project(0, 0, a)
            pe.wait_ge(prep_sb, DC + 5)
            project_c(0, 0)

            def stage_1_rest(a):
                if a < 2:
                    product_G(2 + a)
                elif a == 2:
                    pe.wait_ge(prep_sb, 2 * DC + 3)
                    for e in range(DC):
                        mm = nc.tensor.matmul(bank[6][0:1, :], bias[2][:, e:e + 1], m_right[:, e, :],
                                              start=(e == 0), stop=(e == DC - 1))
                    mm.then_inc(prep_ps, 1)
                else:
                    pe.wait_ge(prep_sb, 2 * DC + 4)
                    nc.tensor.matmul(bank[7][:, :], ones[0:1, :], beta_row, start=True, stop=True
                                     ).then_inc(prep_ps, 1)

            def block_step(nb, j, h, beside=None):
                for a in range(DC):
                    project(nb - 1, 1 - j, a)
                    if beside is not None:
                        beside(a)
                    scan(nb, h, 2 * a)
                    scan(nb, h, 2 * a + 1)
                project_c(nb - 1, 1 - j)

            for nb in range(2, NB // 2):
                block_step(nb, nb % 2, 0, stage_1_rest if nb == 2 else None)
            with strided(pe, NB // 2, NB, 2) as nb:
                for j in range(2):
                    block_step(nb + j, j, 1)

            def spread_slots(r, h):
                for c in range(CH):
                    pe.wait_ge(spread_sb, r * (2 * CH) + (h * CH + c + 1))
                    nc.tensor.matmul(bank[6 + h][:, c * HT:(c + 1) * HT],
                                     spread[:, c, :, :].rearrange("p g s -> p (g s)"), tile_select,
                                     start=True, stop=True).then_inc(spread_ps, 1)

            pe.wait_ge(prep_sb, 2 * DC + 5)
            spread_slots(0, 0)
            for a in range(DC):
                project(NB - 1, 1, a)
            project_c(NB - 1, 1)
            pe.wait_ge(lead_sb, 5)
            nc.tensor.matmul(bank[1][0:1, 0:P], small[:, 42:43], ident, start=True, stop=True).then_inc(lead_ps, 1)
            pe.wait_ge(q_sb, NB * DC + 2)
            pe.wait_ge(c_sb, NB + 2)
            spread_slots(0, 1)

            def attend(r):
                wait_apart(pe, index_ready, r * (4 * CH) + 4 * CH)

                def step(t, third, s, new, mid, old):
                    n, p = r * T + t, s % 2

                    def keys(c):
                        ps = key_bank[c]
                        for a in range(DC):
                            mm = nc.tensor.transpose(ps[:, a * P:(a + 1) * P], kv[:, s % KV, c, a * P:(a + 1) * P],
                                                     ident)
                        mm.then_inc(keyT_ps, 1)

                    def scores(c, stop):
                        pe.wait_ge(keyT_sb, n * (CH - 1) + (stop - 1))
                        for a in range(DC):
                            mm = nc.tensor.matmul(bank[6][:, c * P:stop * P], q_tile[:, a, :],
                                                  keyT[:, a, c * P:stop * P], start=(a == 0), stop=(a == DC - 1))
                        return mm

                    if old:
                        pe.wait_ge(probT_sb, n - 1)
                        if s >= 4:
                            pe.wait_ge(o_sb, n - 3)
                        for c in range(CH):
                            mm = nc.tensor.matmul(bank[2 + p][:, :], probT[:, p, c * P:(c + 1) * P],
                                                  kv[:, (s - 2) % KV, c, D:2 * D], start=(c == 0), stop=(c == CH - 1))
                        mm.then_inc(pv_ps, 1)
                    if new:
                        items = r * IN_BUF[s % KV] + (third + 1)
                        pe.wait_ge(gathered[s % KV], items * (16 * CH))
                        for c in range(CH):
                            keys(c)
                        pe.wait_ge(adj_gathered[s % KV], items * (16 * CH))
                        if s >= 1:
                            pe.wait_ge(adjT_sb, n)
                        for c in range(CH):
                            mm = nc.tensor.transpose(bank[0][:, c * P:(c + 1) * P], adj_g[:, s % KV, c, :], ident)
                        mm.then_inc(adjT_ps, 1)
                        pe.wait_ge(q_tile_sb, n + 1)
                        pe.wait_ge(keyT0_sb, n + 1)
                        if s >= 1:
                            pe.wait_ge(prod_sb, n)
                        scores(0, CH - 1)
                    if mid:
                        pe.wait_ge(weight_sb, n)
                        if s >= 2:
                            pe.wait_ge(probT_sb, n - 1)
                        for c in range(CH):
                            mm = nc.tensor.transpose(bank[1][:, c * P:(c + 1) * P], score[:, c * P:(c + 1) * P], ident)
                        mm.then_inc(probT_ps, 1)
                    if new:
                        scores(CH - 1, CH).then_inc(score_ps, 1)

                return step

            def sum_values():
                pe.wait_ge(v_added, 2 + 2 * NB)
                pe.wait_ge(o_sb, 17)
                for k in range(2):
                    mm = nc.tensor.matmul(bank[2][:, :], ones[:, :], v_acc[:, k * D:(k + 1) * D],
                                          start=(k == 0), stop=(k == 1))
                mm.then_inc(vsum_ps, 1)
                pe.wait_ge(vsum_sb, 1)

            first_tile_steps(pe, attend(0), sum_values)
            with more_rounds(pe) as r:
                spread_slots(r, 0)
                spread_slots(r, 1)
                tile_steps(pe, attend(r))

            def out_step(t, s, new, old):
                if new:
                    pe.wait_ge(on_sb, t + 1)
                    if s >= 2:
                        pe.wait_ge(onT_sb, t - 1)
                    for a in range(DC):
                        mm = nc.tensor.transpose(bank[4 + s % 2][:, a * P:(a + 1) * P],
                                                 on_buf[s % 2][:, a * P:(a + 1) * P], ident)
                    mm.then_inc(onT_ps, 1)
                if old:
                    pe.wait_ge(onT_sb, t)
                    if s >= 3:
                        pe.wait_ge(y_sb, t - 2)
                    for a in range(DC):
                        mm = nc.tensor.matmul(bank[6 + s % 2][:, :], onT_buf[(s - 1) % 2][:, a, :], G[:, a, :],
                                              start=(a == 0), stop=(a == DC - 1))
                    mm.then_inc(y_ps, 1)

            for t in range(4):
                out_step(t, t, True, t >= 1)
            with strided(pe, 4, T, 4) as t:
                for j in range(4):
                    out_step(t + j, 4 + j, True, True)
            out_step(T, 4, False, True)

        @block.scalar
        def _(act):
            act.sem_inc(q_sb, 2)
            act.sem_inc(c_sb, 2)
            act.wait_ge(prep_sb, DC + 3)
            with strided(act, 0, NB, 2) as nb:
                for j in range(2):
                    for a in range(DC):
                        act.wait_ge(q_ps, nb * DC + (DC * j + a + 1))
                        nc.scalar.activation(cols(qT[:, a, :], nb * 512 + 512 * j, 512), bank[2 + a % 2][:, :],
                                             ACT.Identity, bias=u_col[:, a:a + 1]).then_inc(q_sb, 1)
                    act.wait_ge(c_ps, nb + (j + 3))
                    nc.scalar.activation(cols(c_cols, nb * 4 + 4 * j, 4), bank[4 + j][:, 0:4],
                                         ACT.Identity, bias=kappa).then_inc(c_sb, 1)

            def attend(r, first):
                def step(t, third, s, new, mid, old):
                    n, p = r * T + t, s % 2

                    def copy_keys(c):
                        act.wait_ge(keyT_ps, n * CH + (c + 1))
                        nc.scalar.activation(keyT[:, :, c * P:(c + 1) * P],
                                             key_bank[c][:, :].rearrange("p (a k) -> p a k", a=DC),
                                             ACT.Copy).then_inc(keyT_sb, 1)

                    if mid:
                        act.wait_ge(prod_sb, n)
                        nc.scalar.activation(size, score, ACT.Abs).then_inc(abs_sb, 1)
                    if new:
                        if s >= 1:
                            act.wait_ge(score_ps, n)
                        nc.scalar.activation(q_tile, qT[:, :, bass.ds(t * P, P)], ACT.Copy).then_inc(q_tile_sb, 1)
                        copy_keys(1)
                    if mid:
                        q = 1 - p
                        act.wait_ge(new_max_sb, n)
                        if not first:
                            nc.scalar.activation(alpha[:, q:q + 1], cols(neg_max, t - 1, 1), ACT.Exp,
                                                 bias=new_max[:, q:q + 1], scale=-1.0).then_inc(alpha_sb, 1)
                        nc.scalar.activation(p_rest[:, q:q + 1], cst[:, C_NEG:C_NEG + 1], ACT.Exp,
                                             bias=new_max[:, q:q + 1]).then_inc(exp_sb, 1)
                        nc.scalar.activation(score, score, ACT.Exp, bias=new_max[:, q:q + 1],
                                             accum_out=p_sum[:, q:q + 1]).then_inc(exp_sb, 1)
                    if new:
                        copy_keys(2)
                    if mid:
                        act.wait_ge(probT_ps, n)
                        if s >= 3:
                            act.wait_ge(pv_ps, n - 2)
                        nc.scalar.activation(probT[:, q, :], bank[1][:, 0:SLOTS], ACT.Copy).then_inc(probT_sb, 1)

                return step

            first_tile_steps(act, attend(0, True), lambda: None)
            with more_rounds(act) as r:
                tile_steps(act, attend(r, False))
            act.wait_ge(rest_sb, 1)
            nc.scalar.activation(p_all, neg_max[:, :], ACT.Exp, bias=cst[:, C_NEG:C_NEG + 1]).then_inc(end_exp, 1)

            def out_step(t, s, new, old):
                if new:
                    act.wait_ge(onT_ps, t + 1)
                    if s >= 2:
                        act.wait_ge(y_ps, t - 1)
                    nc.scalar.activation(onT_buf[s % 2].rearrange("p a r -> p (a r)"), bank[4 + s % 2][:, :], ACT.Copy
                                         ).then_inc(onT_sb, 1)
                if old:
                    act.wait_ge(mean_sb, t - 1)
                    nc.scalar.activation(std[:, s % 2:s % 2 + 1], mean_var[:, s % 2, 1:2], ACT.Sqrt,
                                         bias=cst[:, C_EPS:C_EPS + 1]).then_inc(std_sb, 1)

            for t in range(4):
                out_step(t, t, True, t >= 2)
            with strided(act, 4, T, 4) as t:
                for j in range(4):
                    out_step(t + j, 4 + j, True, True)
            out_step(T, 4, False, True)
            out_step(T + 1, 5, False, True)

        @block.vector
        def _(dve):
            dve.sem_inc(joined_sb, 4)
            dve.sem_inc(v_added, 2)
            dve.sem_inc(stored[0], 16)
            dve.sem_inc(stored[1], 16)
            nc.vector.memset(ones[:, :], 1.0).then_inc(filled, 1)
            nc.vector.memset(one_hot, 0.0).then_inc(filled, 1)
            dve.wait_ge(filled, 2)
            nc.vector.memset(one_hot[:, 127:128], 1.0).then_inc(filled, 1)
            dve.wait_ge(cst_in, 16)
            nc.vector.tensor_tensor(small[:, 0:DC], cst[:, C_B:C_B + DC], cst[:, C_B + DC:C_B + 2 * DC], ALU.mult
                                    ).then_inc(filled, 1)

            def join(k, i):
                dve.wait_ge(adj_in[i], (k - i) * 4 + 16)
                dve.wait_ge(joined_used, k + 1)
                nc.vector.tensor_scalar(joined[i % 2], adj_buf[i], 0.0, None, ALU.not_equal
                                        ).then_inc(joined_sb, 1)

            def project_c(nb, j):
                dve.wait_ge(xT_in[j], nb * 8 + (16 - 8 * j))
                dve.wait_ge(prep_sb, DC + 3)
                dve.wait_ge(c_ps, nb + 2)
                for d in range(DC):
                    if d == 0:
                        nc.vector.tensor_scalar(c_part, xT_buf[j][:, d, :], w_col[:, d:d + 1], None, ALU.mult
                                                ).then_inc(c_part_sb, 1)
                    else:
                        dve.wait_ge(c_part_sb, nb * DC + d)
                        nc.vector.scalar_tensor_tensor(c_part, xT_buf[j][:, d, :], w_col[:, d:d + 1], c_part,
                                                       ALU.mult, ALU.add).then_inc(c_part_sb, 1)

            def join_block(nb, j, between=None):
                for i in range(8):
                    join(nb * 8 + i, i % 4)
                    if i == 4:
                        project_c(nb - 1, 1 - j)
                    if between is not None:
                        between(i)

            join(0, 0)
            for a in range(DC):
                join(a + 1, (a + 1) % 4)
                dve.wait_ge(prep_ps, a + 1)
                nc.vector.tensor_scalar(M[:, a, :], bank[4 + a][:, :], INV_SCALE, None, ALU.mult).then_inc(prep_sb, 1)
            for k in range(DC + 1, 2 * DC + 1):
                join(k, k % 4)
            dve.wait_ge(prep_ps, DC + 2)
            nc.vector.tensor_scalar(u_col, bank[2][:, 0:DC], INV_SCALE, None, ALU.mult).then_inc(prep_sb, 1)
            nc.vector.tensor_scalar(w_col, bank[2][:, DC:2 * DC], INV_SCALE, None, ALU.mult).then_inc(prep_sb, 1)
            dve.wait_ge(prep_ps, DC + 3)
            nc.vector.tensor_scalar(small[:, 8:8 + DC], bank[3][:, 0:DC], INV_SCALE, 0.0, ALU.mult, ALU.add,
                                    accum_out=kappa).then_inc(prep_sb, 1)
            def copy_G(a):
                dve.wait_ge(prep_ps, DC + 4 + a)
                nc.vector.tensor_copy(G[:, a, :], bank[4 + a][:, :]).then_inc(prep_sb, 1)

            join(9, 1)
            for a in range(DC):
                if a < DC - 1:
                    for k in (2 * a + 2, 2 * a + 3):
                        join(8 + k, k % 4)
                if a == 2:
                    project_c(0, 0)
                if a < 2:
                    copy_G(a)

            def stage_1_rest(i):
                if i in (1, 3):
                    copy_G(2 + i // 2)
                if i == 5:
                    dve.wait_ge(prep_ps, 2 * DC + 4)
                    dve.wait_ge(bm_in, 16)
                    nc.vector.tensor_tensor(beta_row, bank[6][0:1, :], bm_row, ALU.add).then_inc(prep_sb, 1)
                if i == 7:
                    dve.wait_ge(prep_ps, 2 * DC + 5)
                    nc.vector.tensor_copy(beta[:, :], bank[7][:, :]).then_inc(prep_sb, 1)

            def number_joined(h):
                dve.wait_ge(joined_used, (h + 1) * (HALVES // 2) + 2)
                nc.vector.scalar_tensor_tensor(left[:, h, :], bank[h][:, :], 0.0, descending, ALU.is_gt, ALU.mult
                                               ).then_inc(lead_sb, 1)
                dve.wait_ge(lead_sb, 2 * h + 1)
                nc.vector.tensor_scalar(bank[h][:, :], left[:, h, :], 0.0, 0.0, ALU.is_gt, ALU.add,
                                        accum_out=small[:, 40 + h:41 + h]).then_inc(lead_sb, 1)
                dve.wait_ge(lead_sb, 2 * h + 2)

            def take_8(r, h, i):
                if i >= GS // 8:
                    return
                k = h * (TAKES // 2) + 2 * i
                found = slots[:, h, 8 * i:8 * i + 8]
                if k:
                    wait_apart(dve, took, r * TAKES + k)
                nc.vector.max(found, left[:, h, :]).then_inc(took, 1)
                wait_apart(dve, took, r * TAKES + (k + 1))
                nc.vector.match_replace(left[:, h, :], found, left[:, h, :], 0.0).then_inc(took, 1)

            def spread_out(h):
                for c in range(CH):
                    nc.vector.tensor_tensor(spread[:, c, :, :], group_mask,
                                            slots[:, h, c * SPC:(c + 1) * SPC].unsqueeze(1)
                                            .broadcast_to([P, G8, SPC]), ALU.mult).then_inc(spread_sb, 1)

            def take(r, h):
                for i in range(GS // 8):
                    take_8(r, h, i)
                spread_out(h)

            def index_slots(r, h):
                dve.wait_ge(spread_ps, r * (2 * CH) + (h + 1) * CH)
                tiles = slice(h * HT, (h + 1) * HT)
                for c in range(CH):
                    v = bank[6 + h][:, c * HT:(c + 1) * HT]
                    nc.vector.tensor_scalar(index[:, tiles, c], v, -float(G8), cst[:, C_BK:C_BK + 1],
                                            ALU.mult, ALU.add).then_inc(index_ready, 1)
                    nc.vector.scalar_tensor_tensor(index[:, tiles, CH + c], v, -float(G8 * T),
                                                   cst[:, C_BA + h * HT:C_BA + (h + 1) * HT],
                                                   ALU.mult, ALU.add).then_inc(index_ready, 1)

            for nb in range(2, NB // 2):
                join_block(nb, nb % 2, stage_1_rest if nb == 2 else None)
            number_joined(0)
            join_block(NB // 2, 0, lambda i: take_8(0, 0, i))
            spread_out(0)
            for nb in range(NB // 2 + 1, NB):
                join_block(nb, nb % 2)
            index_slots(0, 0)
            project_c(NB - 1, 1)
            number_joined(1)
            nc.vector.tensor_tensor(small[:, 42:43], small[:, 40:41], small[:, 41:42], ALU.max).then_inc(lead_sb, 1)
            take(0, 1)
            dve.wait_ge(lead_ps, 1)
            nc.vector.tensor_reduce(small[0:1, 43:44], bank[1][0:1, 0:P], AX_X, ALU.max).then_inc(lead_sb, 1)
            index_slots(0, 1)
            dve.wait_ge(lead_sb, 6)
            nc.vector.tensor_scalar(small[0:1, 44:44 + MAXR - 1], cst[0:1, C_THR:C_THR + MAXR - 1], small[0:1, 43:44],
                                    0.0, ALU.is_lt, ALU.add, accum_out=small[0:1, 60:61]).then_inc(lead_sb, 1)
            dve.wait_ge(lead_sb, 7)
            nc.vector.tensor_copy(rounds_i[:, :], small[0:1, 60:61]).then_inc(rounds_ready, 1)

            dve.wait_ge(c_sb, NB + 2)
            dve.wait_ge(c_ps, NB + 2)
            nc.vector.memset(v_acc, 0.0).then_inc(v_zeroed, 1)
            dve.wait_ge(v_zeroed, 1)

            def attend(r, first):
                def step(t, third, s, new, mid, old):
                    n, p = r * T + t, s % 2
                    if mid:
                        q = 1 - p
                        dve.wait_ge(score_ps, n)
                        dve.wait_ge(adjT_sb, n)
                        nc.vector.scalar_tensor_tensor(score, bank[6][:, 0:SLOTS], cols(c_cols, t - 1, 1),
                                                       adjT[:, :], ALU.add, ALU.mult).then_inc(prod_sb, 1)
                        dve.wait_ge(abs_sb, n)
                        nc.vector.tensor_scalar(size, size, TINY, MASKED, ALU.is_lt, ALU.mult).then_inc(tiny_sb, 1)
                        dve.wait_ge(tiny_sb, n)
                        nc.vector.tensor_tensor(score, score, size, ALU.add).then_inc(masked, 1)
                        dve.wait_ge(masked, n)
                        nc.vector.tensor_reduce(chunk_max[:, q:q + 1], score, AX_X, ALU.max, negate=True
                                                ).then_inc(max_sb, 1)
                        dve.wait_ge(max_sb, n)
                        if first:
                            nc.vector.tensor_scalar(new_max[:, q:q + 1], chunk_max[:, q:q + 1], -MASKED, None,
                                                    ALU.min).then_inc(new_max_sb, 1)
                        else:
                            nc.vector.tensor_tensor(new_max[:, q:q + 1], chunk_max[:, q:q + 1],
                                                    cols(neg_max, t - 1, 1), ALU.min).then_inc(new_max_sb, 1)
                    if new:
                        dve.wait_ge(keyT_ps, n * CH + 1)
                        nc.vector.tensor_copy(keyT[:, :, 0:P], key_bank[0][:, :].rearrange("p (a k) -> p a k", a=DC)
                                              ).then_inc(keyT0_sb, 1)
                        dve.wait_ge(adjT_ps, n + 1)
                        if s >= 1:
                            dve.wait_ge(prod_sb, n)
                        nc.vector.tensor_copy(adjT[:, :], bank[0][:, 0:SLOTS]).then_inc(adjT_sb, 1)
                    if mid:
                        dve.wait_ge(exp_sb, n * 2)
                        nc.vector.tensor_scalar(score, score, p_rest[:, q:q + 1], None, ALU.subtract
                                                ).then_inc(weight_sb, 1)
                        l = cols(denom, t - 1, 1)
                        nc.vector.scalar_tensor_tensor(l if first else l_add[:, q:q + 1], p_rest[:, q:q + 1],
                                                       -float(SLOTS), p_sum[:, q:q + 1], ALU.mult, ALU.add
                                                       ).then_inc(denom_sb if first else sum_sb, 1)
                        if not first:
                            dve.wait_ge(alpha_sb, n - T)
                            dve.wait_ge(sum_sb, n - T)
                            nc.vector.scalar_tensor_tensor(l, l, alpha[:, q:q + 1], l_add[:, q:q + 1],
                                                           ALU.mult, ALU.add).then_inc(denom_sb, 1)
                        nc.vector.tensor_copy(cols(neg_max, t - 1, 1), new_max[:, q:q + 1]).then_inc(state_sb, 1)
                    if old:
                        dve.wait_ge(pv_ps, n - 1)
                        acc = O[:, bass.ds(t - 2, 1), :].rearrange("p a d -> p (a d)")
                        if first:
                            nc.vector.tensor_copy(acc, bank[2 + p][:, :]).then_inc(o_sb, 1)
                        else:
                            nc.vector.scalar_tensor_tensor(acc, acc, alpha[:, p:p + 1], bank[2 + p][:, :],
                                                           ALU.mult, ALU.add).then_inc(o_sb, 1)
                    if first and new and 2 <= s < 2 + 2 * NB:
                        dve.wait_ge(v_in[p], t * 8 - 8 * p)
                        dve.wait_ge(v_added, t)
                        nc.vector.tensor_tensor(v_acc, v_acc, v_buf[p], ALU.add).then_inc(v_added, 1)

                return step

            def copy_sum():
                dve.wait_ge(vsum_ps, 1)
                nc.vector.tensor_copy(vsum[:, :], bank[2][:, :]).then_inc(vsum_sb, 1)

            def settle(r):
                dve.wait_ge(o_sb, r * T + T)
                dve.wait_ge(denom_sb, r * T + T)
                dve.wait_ge(state_sb, r * T + T)

            first_tile_steps(dve, attend(0, True), copy_sum)
            settle(0)
            with more_rounds(dve) as r:
                for h in range(2):
                    take(r, h)
                    index_slots(r, h)
                tile_steps(dve, attend(r, False))
                settle(r)
            dve.sem_inc(rest_sb, 1)
            dve.sem_inc(end_sb, 1)
            dve.wait_ge(end_exp, 1)

            def out_step(t, s, new, mid, old):
                if new:
                    if s >= 2:
                        dve.wait_ge(onT_ps, t - 1)
                    nc.vector.scalar_tensor_tensor(on_buf[s % 2], vsum[:, :], cols(p_all, t, 1),
                                                   O[:, bass.ds(t, 1), :].rearrange("p a d -> p (a d)"),
                                                   ALU.mult, ALU.add).then_inc(on_sb, 1)
                if mid:
                    b = s % 2
                    dve.wait_ge(y_ps, t - 1)
                    dve.wait_ge(xb_sb, t - 1)
                    if s >= 4:
                        dve.wait_ge(fin_sb, t - 3)
                    nc.vector.scalar_tensor_tensor(y_buf[b], bank[6 + (s + 1) % 2][:, :], cols(r_denom, t - 2, 1),
                                                   x_buf[(s - 2) % 4], ALU.mult, ALU.add).then_inc(y_sb, 1)
                    dve.wait_ge(y_sb, t - 1)
                    nc.vector.bn_stats(stats[:, b, :], y_buf[b]).then_inc(stats_sb, 1)
                    wait_apart(dve, stats_sb, t - 1)
                    nc.vector.bn_aggr(mean_var[:, b, :], stats[:, b, :]).then_inc(mean_sb, 1)
                if old:
                    b = (s - 3) % 2
                    dve.wait_ge(std_sb, t - 2)
                    nc.vector.reciprocal(rstd[:, b:b + 1], std[:, b:b + 1]).then_inc(rstd_sb, 1)
                    dve.wait_ge(rstd_sb, t - 2)
                    dve.wait_ge(stored[b], (t - s) * 8 + (16 * ((s - 3) // 2) + 16))
                    nc.vector.tensor_scalar(fin_buf[b], y_buf[b], mean_var[:, b, 0:1], rstd[:, b:b + 1],
                                            ALU.subtract, ALU.mult).then_inc(fin_sb, 1)

            for t in range(2):
                out_step(t, t, True, False, False)
            nc.vector.scalar_tensor_tensor(denom[:, :], p_all, float(N), denom[:, :], ALU.mult, ALU.add
                                           ).then_inc(end_l, 1)
            dve.wait_ge(end_l, 1)
            nc.vector.reciprocal(r_denom[:, :], denom[:, :]).then_inc(end_l, 1)
            dve.wait_ge(end_l, 2)
            for t in range(2, 4):
                out_step(t, t, True, True, t >= 3)
            with strided(dve, 4, T, 4) as t:
                for j in range(4):
                    out_step(t + j, 4 + j, True, True, True)
            for t in range(T, T + 3):
                out_step(t, t, False, t < T + 2, True)


def layout(adj, key, value, x, Wq, Wk, Wv, Wm, bq, bk, bv, bm):
    import numpy as np

    a = adj.reshape(P, T, GK, 2, G8 // 2)
    const = np.zeros((P, C_ALL), np.float32)
    p = np.arange(P)
    const[:, C_ID:C_ID + P] = np.eye(P)
    const[:, C_DESC:C_DESC + GK] = GK - np.arange(GK)
    const[:, C_GRP:C_GRP + P] = (p % G8)[:, None] == (p // SPC)[None, :]
    const[:, C_SEL:C_SEL + HT] = (p // G8)[:, None] == np.arange(HT)[None, :]
    const[:, C_BK] = N + p // SPC
    const[:, C_BA:C_BA + T] = (T * (N + p // SPC))[:, None] + np.arange(T)[None, :]
    const[:, C_THR:C_THR + MAXR - 1] = [GS * q for q in range(1, MAXR)]
    const[:, C_NEG] = MASKED
    const[:, C_EPS] = 1e-5
    for i, b in enumerate((bq, bk, bv)):
        const[:, C_B + i * DC:C_B + (i + 1) * DC] = b.reshape(DC, P).T
    return {
        "adj_tiles": np.ascontiguousarray(a.transpose(1, 3, 0, 4, 2)).reshape(HALVES, P, N // 2),
        "adj_cols": np.concatenate([adj.reshape(P, T, N).transpose(2, 1, 0).reshape(N * T, P),
                                    np.zeros((G8 * T, P), adj.dtype)]),
        "kv_rows": np.concatenate([key, value], axis=1),
        "value": value,
        "x": x,
        "xT": np.ascontiguousarray(x.reshape(P, NB, T // NB, DC, P).transpose(1, 4, 3, 2, 0)).reshape(NB, P, DC, 512),
        "wq": Wq, "wk": Wk, "wv": Wv, "wmT": np.ascontiguousarray(Wm.T),
        "bm": bm.reshape(1, D),
        "consts": const,
    }


def kernel(x, adj, L0_gnn_key, L0_gnn_value, L0_gnn_Wq, L0_gnn_bq, L0_gnn_Wk, L0_gnn_bk, L0_gnn_Wv, L0_gnn_bv,
           L0_gnn_Wm, L0_gnn_bm):
    import numpy as np
    import concourse.bacc as bacc
    from concourse.bass_utils import run_bass_kernel_spmd

    given = [np.asarray(i) for i in (adj, L0_gnn_key, L0_gnn_value, x, L0_gnn_Wq, L0_gnn_Wk, L0_gnn_Wv, L0_gnn_Wm,
                                     L0_gnn_bq, L0_gnn_bk, L0_gnn_bv, L0_gnn_bm)]
    arrays = layout(*given)
    nc = bacc.Bacc("TRN2", target_bir_lowering=False, num_devices=1)
    args = {n: nc.dram_tensor(n, a.shape, mybir.dt.from_np(a.dtype), kind="ExternalInput").ap()
            for n, a in arrays.items()}
    out = nc.dram_tensor("out", (N, D), F32, kind="ExternalOutput").ap()
    build(nc, out=out, **args)
    r = run_bass_kernel_spmd(nc, [arrays], core_ids=[0])
    return r.results[0]["out"]
```
